# Optimizing a Trainium2 kernel written in Bass

```python
import numpy as np
import jax
import jax.numpy as jnp

def _softmax(x, axis=-1):
    return jax.nn.softmax(x, axis=axis)

def _gelu(x):
    return jax.nn.gelu(x, approximate=True)

def _silu(x):
    return jax.nn.silu(x)

def _sigmoid(x):
    return jax.nn.sigmoid(x)

def _layernorm(x, axis=-1, eps=1e-05):
    m = jnp.mean(x, axis=axis, keepdims=True)
    v = jnp.var(x, axis=axis, keepdims=True)
    return (x - m) / jnp.sqrt(v + eps)

def _scatter_add(tgt, idx, src, axis=0):
    return tgt.at[idx].add(src)

def _segment_sum(src, seg, n):
    return jax.ops.segment_sum(src, seg, n)
kernel_name = 'mk_hybrid_d1_jaxref_r8_5d40c2'

def setup_inputs(seed: int=0):
    np.random.seed(seed)
    _w = jnp.asarray

    def _L0_attn_a_setup():
        import jax, jax.numpy as jnp
        import numpy as np
        N_HEAD = 16
        GAMMA_MIN = 0.9
        GAMMA_MAX = 0.999
        GN_EPS = 1e-05

        def _gammas(n_head):
            lo = float(np.log(1.0 - GAMMA_MAX))
            hi = float(np.log(1.0 - GAMMA_MIN))
            return 1.0 - jnp.exp(jnp.linspace(lo, hi, n_head, dtype=jnp.float32))
        key = jax.random.key(seed)
        ks = jax.random.split(key, 5)
        B, T, C = (2, 256, 128)
        scale = 0.02
        return {'x': jax.random.normal(ks[0], (B, T, C), dtype=jnp.float32), 'wq': jax.random.normal(ks[1], (C, C), dtype=jnp.float32) * scale, 'wk': jax.random.normal(ks[2], (C, C), dtype=jnp.float32) * scale, 'wv': jax.random.normal(ks[3], (C, C), dtype=jnp.float32) * scale, 'wo': jax.random.normal(ks[4], (C, C), dtype=jnp.float32) * scale, 'gn_w': jnp.ones((C,), dtype=jnp.float32), 'gn_b': jnp.zeros((C,), dtype=jnp.float32)}
    _L0_attn_a_in = _L0_attn_a_setup()

    def _L0_attn_b_setup():
        import jax, jax.numpy as jnp
        import numpy as np
        B, L, D = (4, 512, 128)

        def hippo_freqs(dim):
            n = np.arange(dim, dtype=np.float32)
            f = np.sqrt(2 * n + 1)
            f = f / f.max()
            return np.exp(-f * np.log(1250)).astype(np.float32)

        def _proj(z):
            mean = z.mean(axis=-1, keepdims=True)
            var = ((z - mean) ** 2).mean(axis=-1, keepdims=True)
            return (z - mean) / (jnp.sqrt(var) + 1e-06)
        key = jax.random.key(seed)
        ks = jax.random.split(key, 8)
        s = 1.0 / np.sqrt(D)
        return {'x': jax.random.normal(ks[0], (B, L, D), dtype=jnp.float32), 'omega': jnp.asarray(hippo_freqs(D)), 'log_gamma': jax.random.normal(ks[1], (D,), dtype=jnp.float32) - 3.0, 'dt': jnp.float32(0.1), 'W_psi': jax.random.uniform(ks[2], (2 * D, D), jnp.float32, -s, s), 'b_psi': jax.random.uniform(ks[3], (2 * D,), jnp.float32, -s, s), 'W_phi': jax.random.uniform(ks[4], (2 * D, D), jnp.float32, -s, s), 'b_phi': jax.random.uniform(ks[5], (2 * D,), jnp.float32, -s, s), 'W_gate': jax.random.uniform(ks[6], (D, D), jnp.float32, -s, s), 'b_gate': jax.random.uniform(ks[7], (D,), jnp.float32, -s, s)}
    _L0_attn_b_in = _L0_attn_b_setup()

    def _L0_ffn_setup():
        import jax, jax.numpy as jnp
        import numpy as np
        from jax import lax
        N_HEADS = 16
        TOP_K = 2
        N_EXPERTS = 8

        def layer_norm(x, w, b, eps=1e-05):
            mu = jnp.mean(x, axis=-1, keepdims=True)
            var = jnp.mean(jnp.square(x - mu), axis=-1, keepdims=True)
            return (x - mu) * lax.rsqrt(var + eps) * w + b

        def attention(x, w_qkv, b_qkv, w_o, b_o):
            B, T, D = x.shape
            dh = D // N_HEADS
            qkv = x @ w_qkv + b_qkv
            q, k, v = jnp.split(qkv, 3, axis=-1)
            q = q.reshape(B, T, N_HEADS, dh)
            k = k.reshape(B, T, N_HEADS, dh)
            v = v.reshape(B, T, N_HEADS, dh)
            scores = jnp.einsum('bqhd,bkhd->bhqk', q, k) / jnp.sqrt(jnp.float32(dh)).astype(x.dtype)
            probs = jax.nn.softmax(scores, axis=-1)
            ctx = jnp.einsum('bhqk,bkhd->bqhd', probs, v).reshape(B, T, D)
            return ctx @ w_o + b_o

        def moe_ff(x, w_gate, w1, b1, w2, b2):
            B, T, D = x.shape
            t = x.reshape(B * T, D)
            probs = jax.nn.softmax(t @ w_gate, axis=-1)
            tw, ti = lax.top_k(probs, TOP_K)
            tw = tw / jnp.sum(tw, axis=-1, keepdims=True)
            out = jnp.zeros_like(t)
            for e in range(N_EXPERTS):
                we = jnp.sum(jnp.where(ti == e, tw, 0.0), axis=-1)
                h = jax.nn.gelu(t @ w1[e] + b1[e]) @ w2[e] + b2[e]
                out = out + we[:, None] * h
            return out.reshape(B, T, D)
        key = jax.random.key(seed)
        ks = jax.random.split(key, 8)
        B, T, D, H, E = (4, 64, 128, 512, 8)
        s = lambda d: 1.0 / np.sqrt(d)
        return {'x': jax.random.normal(ks[0], (B, T, D), jnp.float32), 'ln1_w': jnp.ones((D,), jnp.float32), 'ln1_b': jnp.zeros((D,), jnp.float32), 'ln2_w': jnp.ones((D,), jnp.float32), 'ln2_b': jnp.zeros((D,), jnp.float32), 'w_qkv': jax.random.normal(ks[1], (D, 3 * D), jnp.float32) * s(D), 'b_qkv': jnp.zeros((3 * D,), jnp.float32), 'w_o': jax.random.normal(ks[2], (D, D), jnp.float32) * s(D), 'b_o': jnp.zeros((D,), jnp.float32), 'w_gate': jax.random.normal(ks[3], (D, E), jnp.float32) * s(D), 'w1': jax.random.normal(ks[4], (E, D, H), jnp.float32) * s(D), 'b1': jnp.zeros((E, H), jnp.float32), 'w2': jax.random.normal(ks[5], (E, H, D), jnp.float32) * s(H), 'b2': jnp.zeros((E, D), jnp.float32)}
    _L0_ffn_in = _L0_ffn_setup()
    _d = {'L0_attn_a_x': _L0_attn_a_in['x'], 'L0_attn_a_wq': _L0_attn_a_in['wq'], 'L0_attn_a_wk': _L0_attn_a_in['wk'], 'L0_attn_a_wv': _L0_attn_a_in['wv'], 'L0_attn_a_wo': _L0_attn_a_in['wo'], 'L0_attn_a_gn_w': _L0_attn_a_in['gn_w'], 'L0_attn_a_gn_b': _L0_attn_a_in['gn_b'], 'L0_attn_b_omega': _L0_attn_b_in['omega'], 'L0_attn_b_log_gamma': _L0_attn_b_in['log_gamma'], 'L0_attn_b_dt': _L0_attn_b_in['dt'], 'L0_attn_b_W_psi': _L0_attn_b_in['W_psi'], 'L0_attn_b_b_psi': _L0_attn_b_in['b_psi'], 'L0_attn_b_W_phi': _L0_attn_b_in['W_phi'], 'L0_attn_b_b_phi': _L0_attn_b_in['b_phi'], 'L0_attn_b_W_gate': _L0_attn_b_in['W_gate'], 'L0_attn_b_b_gate': _L0_attn_b_in['b_gate'], 'L0_ffn_ln1_w': _L0_ffn_in['ln1_w'], 'L0_ffn_ln1_b': _L0_ffn_in['ln1_b'], 'L0_ffn_ln2_w': _L0_ffn_in['ln2_w'], 'L0_ffn_ln2_b': _L0_ffn_in['ln2_b'], 'L0_ffn_w_qkv': _L0_ffn_in['w_qkv'], 'L0_ffn_b_qkv': _L0_ffn_in['b_qkv'], 'L0_ffn_w_o': _L0_ffn_in['w_o'], 'L0_ffn_b_o': _L0_ffn_in['b_o'], 'L0_ffn_w_gate': _L0_ffn_in['w_gate'], 'L0_ffn_w1': _L0_ffn_in['w1'], 'L0_ffn_b1': _L0_ffn_in['b1'], 'L0_ffn_w2': _L0_ffn_in['w2'], 'L0_ffn_b2': _L0_ffn_in['b2']}
    _x0 = _d['L0_attn_a_x']
    _d['L0_attn_a_x'] = jax.random.normal(jax.random.fold_in(jax.random.key(seed), 1), (16, 512, 128), dtype=_x0.dtype)
    del _x0
    return _d

def reference(L0_attn_a_x, L0_attn_a_wq, L0_attn_a_wk, L0_attn_a_wv, L0_attn_a_wo, L0_attn_a_gn_w, L0_attn_a_gn_b, L0_attn_b_omega, L0_attn_b_log_gamma, L0_attn_b_dt, L0_attn_b_W_psi, L0_attn_b_b_psi, L0_attn_b_W_phi, L0_attn_b_b_phi, L0_attn_b_W_gate, L0_attn_b_b_gate, L0_ffn_ln1_w, L0_ffn_ln1_b, L0_ffn_ln2_w, L0_ffn_ln2_b, L0_ffn_w_qkv, L0_ffn_b_qkv, L0_ffn_w_o, L0_ffn_b_o, L0_ffn_w_gate, L0_ffn_w1, L0_ffn_b1, L0_ffn_w2, L0_ffn_b2):

    def _L0_attn_a_ref(x, wq, wk, wv, wo, gn_w, gn_b):
        import jax, jax.numpy as jnp
        import numpy as np
        N_HEAD = 16
        GAMMA_MIN = 0.9
        GAMMA_MAX = 0.999
        GN_EPS = 1e-05

        def _gammas(n_head):
            lo = float(np.log(1.0 - GAMMA_MAX))
            hi = float(np.log(1.0 - GAMMA_MIN))
            return 1.0 - jnp.exp(jnp.linspace(lo, hi, n_head, dtype=jnp.float32))
        B, T, C = x.shape
        H = N_HEAD
        d = C // H
        gammas = _gammas(H)
        q = (x @ wq.T).reshape(B, T, H, d).transpose(0, 2, 1, 3)
        k = (x @ wk.T).reshape(B, T, H, d).transpose(0, 2, 1, 3)
        v = (x @ wv.T).reshape(B, T, H, d).transpose(0, 2, 1, 3)
        pos = jnp.arange(T, dtype=jnp.float32)
        dist = pos[:, None] - pos[None, :]
        causal = dist >= 0
        safe_dist = jnp.where(causal, dist, 0.0)
        D = jnp.where(causal, gammas[:, None, None] ** safe_dist, 0.0)
        scores = jnp.einsum('bhid,bhjd->bhij', q, k) * D
        y = jnp.einsum('bhij,bhjd->bhid', scores, v)
        y = y.transpose(0, 2, 1, 3)
        mean = y.mean(axis=(1, 3), keepdims=True)
        var = y.var(axis=(1, 3), keepdims=True)
        y = (y - mean) * jax.lax.rsqrt(var + GN_EPS)
        y = y.reshape(B, T, C) * gn_w + gn_b
        return y @ wo.T

    def _L0_attn_b_ref(x, omega, log_gamma, dt, W_psi, b_psi, W_phi, b_phi, W_gate, b_gate):
        import jax, jax.numpy as jnp
        import numpy as np
        B, L, D = (4, 512, 128)

        def hippo_freqs(dim):
            n = np.arange(dim, dtype=np.float32)
            f = np.sqrt(2 * n + 1)
            f = f / f.max()
            return np.exp(-f * np.log(1250)).astype(np.float32)

        def _proj(z):
            mean = z.mean(axis=-1, keepdims=True)
            var = ((z - mean) ** 2).mean(axis=-1, keepdims=True)
            return (z - mean) / (jnp.sqrt(var) + 1e-06)
        Bn, Ln, Dn = x.shape
        psi_raw = jnp.einsum('bld,ed->ble', x, W_psi) + b_psi
        phi_raw = jnp.einsum('bld,ed->ble', x, W_phi) + b_phi
        psi = jax.lax.complex(psi_raw[..., :Dn], psi_raw[..., Dn:])
        phi = jax.lax.complex(phi_raw[..., :Dn], phi_raw[..., Dn:])
        gate = jax.nn.sigmoid(jnp.einsum('bld,ed->ble', x, W_gate) + b_gate)
        U = gate.astype(psi.dtype) * psi
        dt_abs = jnp.abs(dt)
        lam = jax.lax.complex(-jnp.exp(log_gamma), omega)
        t_axis = jnp.arange(Ln, dtype=jnp.float32)
        kernel = jnp.exp(lam[None, :] * t_axis[:, None].astype(lam.dtype) * dt_abs)
        n_fft = 2 * Ln
        Kf = jnp.fft.fft(kernel, n=n_fft, axis=0)
        Uf = jnp.fft.fft(U, n=n_fft, axis=1)
        H = jnp.fft.ifft(Uf * Kf[None], axis=1)[:, :Ln]
        H_proj = jax.lax.complex(_proj(H.real), _proj(H.imag))
        return (H_proj * jnp.conj(phi)).real

    def _L0_ffn_ref(x, ln1_w, ln1_b, ln2_w, ln2_b, w_qkv, b_qkv, w_o, b_o, w_gate, w1, b1, w2, b2):
        import jax, jax.numpy as jnp
        import numpy as np
        from jax import lax
        N_HEADS = 16
        TOP_K = 2
        N_EXPERTS = 8

        def layer_norm(x, w, b, eps=1e-05):
            mu = jnp.mean(x, axis=-1, keepdims=True)
            var = jnp.mean(jnp.square(x - mu), axis=-1, keepdims=True)
            return (x - mu) * lax.rsqrt(var + eps) * w + b

        def attention(x, w_qkv, b_qkv, w_o, b_o):
            B, T, D = x.shape
            dh = D // N_HEADS
            qkv = x @ w_qkv + b_qkv
            q, k, v = jnp.split(qkv, 3, axis=-1)
            q = q.reshape(B, T, N_HEADS, dh)
            k = k.reshape(B, T, N_HEADS, dh)
            v = v.reshape(B, T, N_HEADS, dh)
            scores = jnp.einsum('bqhd,bkhd->bhqk', q, k) / jnp.sqrt(jnp.float32(dh)).astype(x.dtype)
            probs = jax.nn.softmax(scores, axis=-1)
            ctx = jnp.einsum('bhqk,bkhd->bqhd', probs, v).reshape(B, T, D)
            return ctx @ w_o + b_o

        def moe_ff(x, w_gate, w1, b1, w2, b2):
            B, T, D = x.shape
            t = x.reshape(B * T, D)
            probs = jax.nn.softmax(t @ w_gate, axis=-1)
            tw, ti = lax.top_k(probs, TOP_K)
            tw = tw / jnp.sum(tw, axis=-1, keepdims=True)
            out = jnp.zeros_like(t)
            for e in range(N_EXPERTS):
                we = jnp.sum(jnp.where(ti == e, tw, 0.0), axis=-1)
                h = jax.nn.gelu(t @ w1[e] + b1[e]) @ w2[e] + b2[e]
                out = out + we[:, None] * h
            return out.reshape(B, T, D)
        h = x + attention(layer_norm(x, ln1_w, ln1_b), w_qkv, b_qkv, w_o, b_o)
        return h + moe_ff(layer_norm(h, ln2_w, ln2_b), w_gate, w1, b1, w2, b2)
    x = L0_attn_a_x
    x = x + _L0_attn_a_ref(_layernorm(x, axis=-1), L0_attn_a_wq, L0_attn_a_wk, L0_attn_a_wv, L0_attn_a_wo, L0_attn_a_gn_w, L0_attn_a_gn_b)
    x = x + _L0_ffn_ref(_layernorm(x, axis=-1), L0_ffn_ln1_w, L0_ffn_ln1_b, L0_ffn_ln2_w, L0_ffn_ln2_b, L0_ffn_w_qkv, L0_ffn_b_qkv, L0_ffn_w_o, L0_ffn_b_o, L0_ffn_w_gate, L0_ffn_w1, L0_ffn_b1, L0_ffn_w2, L0_ffn_b2)
    x = x + _L0_attn_b_ref(_layernorm(x, axis=-1), L0_attn_b_omega, L0_attn_b_log_gamma, L0_attn_b_dt, L0_attn_b_W_psi, L0_attn_b_b_psi, L0_attn_b_W_phi, L0_attn_b_b_phi, L0_attn_b_W_gate, L0_attn_b_b_gate)
    x = x + _L0_ffn_ref(_layernorm(x, axis=-1), L0_ffn_ln1_w, L0_ffn_ln1_b, L0_ffn_ln2_w, L0_ffn_ln2_b, L0_ffn_w_qkv, L0_ffn_b_qkv, L0_ffn_w_o, L0_ffn_b_o, L0_ffn_w_gate, L0_ffn_w1, L0_ffn_b1, L0_ffn_w2, L0_ffn_b2)
    return x

_drawn_inputs = setup_inputs


def setup_inputs(seed=0):
    import zlib

    import numpy as np

    out = dict(_drawn_inputs(seed))
    spreads = {'L0_attn_a_gn_w': (1.0, 0.2),
     'L0_attn_a_gn_b': (0.0, 0.1),
     'L0_ffn_ln1_w': (1.0, 0.2),
     'L0_ffn_ln1_b': (0.0, 0.1),
     'L0_ffn_ln2_w': (1.0, 0.2),
     'L0_ffn_ln2_b': (0.0, 0.1),
     'L0_ffn_b_qkv': (0.0, 0.1),
     'L0_ffn_b_o': (0.0, 0.1),
     'L0_ffn_b1': (0.0, 0.1),
     'L0_ffn_b2': (0.0, 0.1)}
    factors = {'L0_attn_b_b_gate': 4.261}
    for name, (base, spread) in spreads.items():
        noise = np.random.default_rng([zlib.crc32(name.encode()), seed]).standard_normal(out[name].shape)
        drawn = base * np.exp(spread * noise) if base else spread * noise
        out[name] = jnp.asarray(drawn.astype(out[name].dtype))
    for name, factor in factors.items():
        out[name] = (out[name] * factor).astype(out[name].dtype)
    return out
```

```python
from contextlib import ExitStack

import numpy as np

import concourse.bass as bass
from concourse import mybir

F32 = mybir.dt.float32
F32R = mybir.dt.float32r
I32 = mybir.dt.int32
U32 = mybir.dt.uint32
ALU = mybir.AluOpType
ACT = mybir.ActivationFunctionType
AX_X = mybir.AxisListType.X

B, T, C = 16, 512, 128
P = 128
TT = T // P
NH = 16
DH = C // NH
G = 4
NG = NH // G
HR = P // G
MAX_ROW = 3 * DH
DEN = DH
NE, NHID = 8, 512
HC = NHID // P
EPS = 1e-5
PROJ_EPS = 1e-6
TINY = 1e-30
SCALE = float(1.0 / np.sqrt(np.float32(DH)))
Q_TERMS = (0, 0, 1)
K_TERMS = (0, 1, 0)
RSQRT_MAGIC = float(0x5F3759DF - (1 << 31))
TWO_PI_HI = 6.28125
TWO_PI_LO = float(2 * np.pi - 6.28125)
ROUND = 12582912.0
REST = P * TT * (TT - 1) // 2
LEAD = 5


def shape_constants():
    lo, hi = np.log(np.float32(1.0 - 0.999)), np.log(np.float32(1.0 - 0.9))
    gammas = (1.0 - np.exp(np.linspace(float(lo), float(hi), NH).astype(np.float32))).astype(np.float32)
    pos = np.arange(T, dtype=np.float64)
    g64 = gammas.astype(np.float64)
    q_decay = np.repeat(g64, DH)[:, None] ** pos
    k_decay = np.repeat(g64, DH)[:, None] ** -pos
    causal = (np.arange(P)[None, :] >= np.arange(P)[:, None])
    spread = np.zeros((P, 4, NG, P), np.float32)
    average = np.zeros((P, P), np.float32)
    ones_row = np.zeros((P, 1), np.float32)
    for t in range(NG):
        for g in range(G):
            for d in range(DH):
                for term in range(3):
                    spread[(G * t + g) * DH + d, Q_TERMS[term], t, HR * g + DH * term + d] = 1.0
                    spread[(G * t + g) * DH + d, 2 + K_TERMS[term], t, HR * g + DH * term + d] = 1.0
    for g in range(G):
        average[HR * g:HR * g + DH, HR * g:HR * g + DH] = 1.0 / DH
        ones_row[HR * g + MAX_ROW] = 1.0
    return {
        "c_q_decay": q_decay.astype(np.float32),
        "c_k_decay": k_decay.astype(np.float32),
        "c_causal": causal.astype(np.float32),
        "c_spread": spread.reshape(P, 4 * NG * P),
        "c_average": average,
        "c_ones_row": ones_row,
        "c_identity": np.eye(P, dtype=np.float32),
        "c_experts": np.tile(np.arange(NE, dtype=np.float32), (P, TT)),
        "c_time": np.tile(np.arange(T, dtype=np.float32), (P, 1)),
    }


class Signal:

    def __init__(self, sem, per):
        self.sem, self.per = sem, per

    def at(self, run, k):
        return run * self.per + k


def build(nc, a, out):
    with ExitStack() as ctx:
        def sb(name, shape, dt=F32):
            return ctx.enter_context(nc.sbuf_tensor(name, shape, dt))

        ident = sb("ident", [P, P])
        ident_r = sb("ident_r", [P, P], F32R)
        qk_decay = sb("qk_decay", [P, 2, T])
        causal = sb("causal", [P, P])
        spread = sb("spread", [P, 4, NG, P], F32R)
        average = sb("average", [P, P])
        ones_row = sb("ones_row", [P, 1])
        experts = sb("experts", [P, TT, NE])
        w_ret = sb("w_ret", [P, 3, P])
        wo_ret = sb("wo_ret", [P, NG, P])
        gn_w = sb("gn_w", [P, NG])
        gn_b = sb("gn_b", [P, NG])
        w_qkv = sb("w_qkv", [P, 3, P])
        b_qk = sb("b_qk", [P, 2])
        b_v = sb("b_v", [P, P])
        b_o = sb("b_o", [P, P])
        w_o = sb("w_o", [P, P])
        ln_wb = sb("ln_wb", [P, 4])
        w_gate = sb("w_gate", [P, NE])
        w1_hi = sb("w1_hi", [P, NE, NHID], F32R)
        w1_lo = sb("w1_lo", [P, NE, NHID], F32R)
        b1 = sb("b1", [P, NE * HC])
        w2 = sb("w2", [P, NE * HC, P])
        b2 = sb("b2", [NE, P])
        w_psi = sb("w_psi", [P, 2 * P])
        w_sgate = sb("w_sgate", [P, P])
        w_phi = sb("w_phi", [P, 2 * P])
        b_psi = sb("b_psi", [P, 2])
        nb_sgate = sb("nb_sgate", [P, 1])
        b_phi = sb("b_phi", [P, 2 * P])
        cos_t = sb("cos_t", [P, T])
        sin_t = sb("sin_t", [P, T])
        rate = sb("rate", [P, 1])

        x = sb("x", [P, TT, C])
        z = sb("z", [P, TT, C])
        zn = sb("zn", [P, TT, C])
        h = sb("h", [P, TT, C])
        aT = sb("aT", [P, T])
        qk_hi = sb("qk_hi", [P, 2, T], F32R)
        qk_lo = sb("qk_lo", [P, 2, T], F32R)
        val = sb("val", [P, TT, NH, HR])
        Qs = sb("Qs", [P, NG, T], F32R)
        Km = sb("Km", [P, NH, T], F32R)
        neg_max = sb("neg_max", [P, 2, TT, P], F32R)
        probs = sb("probs", [P, 2, G, T])
        head_out = sb("head_out", [P, NG, T])
        qk_f = head_out[:, 0:2, :]
        rden = sb("rden", [P, TT, G])
        ctxt = z
        ctxT = aT
        stat = sb("stat", [P, 8, 6])
        mv = sb("mv", [P, 8, 2])
        small = sb("small", [P, 8, 8])
        gn = sb("gn", [P, 6, NG])
        tn = zn
        tT = sb("tT", [P, T])
        t_hi = sb("t_hi", [P, T], F32R)
        t_lo = sb("t_lo", [P, T], F32R)
        logits = sb("logits", [P, TT, NE])
        top = sb("top", [P, TT, 8])
        top_i = sb("top_i", [P, TT, 8], U32)
        top_f = sb("top_f", [P, TT, 8])
        gw = sb("gw", [P, 4, TT])
        hot = sb("hot", [P, 2, TT, NE])
        we = sb("we", [P, TT, NE])
        weT = sb("weT", [NE, T])
        r_behind = sb("r_behind", [P, 2, G, REST])
        hid = r_behind[:].rearrange("p a g q -> p (a g q)")[:, 0:2 * HC * T].rearrange(
            "p (a c t) -> p a c t", a=2, c=HC)
        U = [hid[:, 0, i, :] for i in range(2)]
        rot = [hid[:, 0, 2 + i, :] for i in range(2)]
        tmp = [hid[:, 1, i, :] for i in range(2)]
        W = [hid[:, 1, 2 + i, :] for i in range(2)]
        sig = qk_f[:, 0, :]
        phi = probs[:, 0, 0:2, :].rearrange("p a t -> p (a t)").rearrange("p (t e) -> p t e", t=TT)
        Hn = probs[:, 1, 0:2, :].rearrange("p a (t c) -> p a t c", t=TT)

        bank = [ctx.enter_context(nc.psum_tensor(f"bank{i}", [P, T], F32)) for i in range(8)]
        MAX_BANKS = (0, 1, 5)
        S_BANKS = (2, 3, 6)
        X_BANKS = (4, 7)
        SPREAD_BANKS = (4, 6, 7, 2)
        R_BANKS = (0, 1, 2, 3, 5, 6)
        O_BANK = 5

        sems = []

        def sem(name):
            s = ctx.enter_context(nc.semaphore(name))
            return s

        loaded = sem("loaded")
        setup_step = sem("setup_step")
        setup_act = sem("setup_act")
        signals = {}

        def signal(name, per):
            s = sem(name)
            sems.append(s)
            signals[name] = Signal(s, per)
            return signals[name]

        x_in = sem("x_in")
        sems.append(x_in)
        stored_it = sem("stored_it")
        sems.append(stored_it)
        vec_step = sem("vec_step")
        sems.append(vec_step)
        normed = signal("normed", 1)
        normT = signal("normT", 1)
        aT_ready = signal("aT_ready", 1)
        qkv_ready = signal("qkv_ready", 3)
        qk_biased = signal("qk_biased", 2)
        qk_split = signal("qk_split", 2)
        v_ready = signal("v_ready", 1)
        spread_ready = signal("spread_ready", 8)
        q_kept = signal("q_kept", NG)
        k_kept = signal("k_kept", NG)
        k_kept_v = signal("k_kept_v", NG)
        r_scores = signal("r_scores", 3 * NH)
        r_diag = signal("r_diag", NH)
        r_rest = signal("r_rest", 2 * NH)
        r_summed = signal("r_summed", NG)
        r_kept = signal("r_kept", NG)
        gn_local = signal("gn_local", 2)
        gn_mean = signal("gn_mean", 2)
        gn_coef = signal("gn_coef", 1)
        gn_done = signal("gn_done", NG)
        r_out = signal("r_out", 1)
        a_scores = signal("a_scores", NH * TT)
        a_max = signal("a_max", NH * TT)
        a_qm = signal("a_qm", NG)
        a_qm_kept = signal("a_qm_kept", NG)
        a_scoresT = signal("a_scoresT", NH * TT)
        a_exp = signal("a_exp", NH * TT)
        a_pv = signal("a_pv", NG * TT)
        a_kept = signal("a_kept", NG)
        a_outT = signal("a_outT", NG)
        a_ctx = signal("a_ctx", NG)
        a_ctxT = signal("a_ctxT", 1)
        a_ctxT_kept = signal("a_ctxT_kept", 1)
        a_proj = signal("a_proj", 1)
        a_zb = signal("a_zb", 1)
        a_h = signal("a_h", 1)
        a_xh = signal("a_xh", 1)
        m_normed = signal("m_normed", 1)
        m_normT = signal("m_normT", 1)
        m_tT = signal("m_tT", 1)
        m_split = signal("m_split", 1)
        m_logits = signal("m_logits", 1)
        m_gap = signal("m_gap", 1)
        m_gap_exp = signal("m_gap_exp", 1)
        m_we = signal("m_we", 1)
        m_weT = signal("m_weT", 1)
        m_weT_kept = signal("m_weT_kept", 1)
        m_bias = signal("m_bias", 1)
        m_hid = signal("m_hid", NE * HC)
        m_gelu = signal("m_gelu", NE * HC)
        m_out = signal("m_out", NE)
        m_acc = signal("m_acc", NE + 1)
        s_normed = signal("s_normed", 1)
        s_normT = signal("s_normT", 1)
        s_aT = signal("s_aT", 1)
        s_proj = signal("s_proj", 3)
        s_gexp = signal("s_gexp", 1)
        s_u = signal("s_u", 2)
        s_phi = signal("s_phi", 1)
        s_h = signal("s_h", 2)
        s_hT = signal("s_hT", 2)
        x_done = signal("x_done", 1)

        with nc.Block() as block:
            loads = []

            @block.sync
            def _(sp):
                def load(dst, src):
                    loads.append(1)
                    sp.dma_start(dst, src).then_inc(loaded, 16)

                load(ident[:], a["c_identity"])
                load(hid[:, :, :, :].rearrange("p a c t -> p (a c t)")[:, 0:4 * NG * P], a["c_spread"])
                load(probs[:, :, :, :].rearrange("p a g t -> p (a g) t")[:, 0:NE, :],
                     a["L0_ffn_w1"].rearrange("e d h -> d e h"))
                load(qk_decay[:, 0, :], a["c_q_decay"])
                load(qk_decay[:, 1, :], a["c_k_decay"])
                load(causal[:], a["c_causal"])
                load(average[:], a["c_average"])
                load(ones_row[:], a["c_ones_row"])
                load(experts[:].rearrange("p t e -> p (t e)"), a["c_experts"])
                load(zn[:].rearrange("p t c -> p (t c)"), a["c_time"])
                for i, n in enumerate(("wq", "wk", "wv")):
                    load(w_ret[:, i, :], a["L0_attn_a_" + n])
                load(w_qkv[:].rearrange("p a n -> p (a n)"), a["L0_ffn_w_qkv"])
                for i in range(2):
                    load(b_qk[:, i:i + 1], a["L0_ffn_b_qkv"][C * i:C * (i + 1)].rearrange("(p o) -> p o", o=1))
                load(b_v[:], a["L0_ffn_b_qkv"][2 * C:3 * C].partition_broadcast(P))
                load(b_o[:], a["L0_ffn_b_o"].partition_broadcast(P))
                load(b_phi[:], a["L0_attn_b_b_phi"].partition_broadcast(P))
                load(w_o[:], a["L0_ffn_w_o"])
                for i, n in enumerate(("ln1_w", "ln1_b", "ln2_w", "ln2_b")):
                    load(ln_wb[:, i:i + 1], a["L0_ffn_" + n].rearrange("(p o) -> p o", o=1))
                load(w_gate[:], a["L0_ffn_w_gate"])
                load(b1[:], a["L0_ffn_b1"])
                load(w2[:], a["L0_ffn_w2"].rearrange("e (c p) n -> p (e c) n", p=P))
                load(b2[:], a["L0_ffn_b2"])
                load(w_psi[:], a["L0_attn_b_W_psi"])
                load(w_sgate[:], a["L0_attn_b_W_gate"])
                load(w_phi[:], a["L0_attn_b_W_phi"])
                load(b_psi[:], a["L0_attn_b_b_psi"])
                load(small[:, 0, 0:1], a["L0_attn_b_b_gate"].rearrange("(p o) -> p o", o=1))
                load(small[:, 1, 0:1], a["L0_attn_b_omega"].rearrange("(p o) -> p o", o=1))
                load(small[:, 2, 0:1], a["L0_attn_b_log_gamma"].rearrange("(p o) -> p o", o=1))
                load(small[:, 3, 0:1], a["L0_attn_b_dt"].partition_broadcast(P))
                sp.wait_ge(setup_step, 1)
                for g in range(G):
                    rows = slice(HR * g, HR * g + DH)
                    load(wo_ret[rows, :, :],
                         a["L0_attn_a_wo"].rearrange("(t g d) n -> g d t n", g=G, d=DH)[g])
                    load(gn_w[rows, :], a["L0_attn_a_gn_w"][g])
                    load(gn_b[rows, :], a["L0_attn_a_gn_b"][g])
                sp.wait_ge(loaded, 16 * len(loads))

            n_loads = len(loads)

            @block.vector
            def _(dve):
                done = [0]

                def link(ins):
                    done[0] += 1
                    ins.then_inc(setup_step, 1)
                    dve.wait_ge(setup_step, done[0])

                dve.memset(gn_w[:], 0.0)
                dve.memset(gn_b[:], 0.0)
                link(dve.memset(wo_ret[:], 0.0))
                dve.memset(val[:], 0.0)
                dve.memset(Km[:].bitcast(F32), 0.0)
                link(dve.memset(neg_max[:].bitcast(F32), 0.0))
                link(dve.memset(val[:, :, :, DEN:DEN + 1], 1.0))
                dve.wait_ge(loaded, 16 * n_loads)
                dve.tensor_copy(ident_r[:], ident[:])
                dve.tensor_copy(spread[:].rearrange("p a t n -> p (a t n)"),
                                hid[:, :, :, :].rearrange("p a c t -> p (a c t)")[:, 0:4 * NG * P])
                w1_f = probs[:, :, :, :].rearrange("p a g t -> p (a g) t")[:, 0:NE, :]
                link(dve.tensor_copy(w1_hi[:], w1_f))
                link(dve.tensor_tensor(w1_lo[:], w1_f, w1_hi[:].bitcast(F32), ALU.subtract))
                dve.tensor_scalar(nb_sgate[:], small[:, 0, 0:1], -1.0, None, ALU.mult)
                link(dve.tensor_scalar(small[:, 4, 0:1], small[:, 3, 0:1], -1.0, None, ALU.mult))
                link(dve.tensor_tensor(small[:, 4, 0:1], small[:, 4, 0:1], small[:, 3, 0:1], ALU.max))
                ang, turns, red = zn[:].rearrange("p t c -> p (t c)"), aT[:], tT[:]
                link(dve.tensor_scalar(ang, ang, small[:, 1, 0:1], small[:, 4, 0:1], ALU.mult, ALU.mult))
                link(dve.tensor_scalar(turns, ang, 1.0 / (2 * np.pi), None, ALU.mult))
                link(dve.tensor_scalar(turns, turns, ROUND, None, ALU.add))
                link(dve.tensor_scalar(turns, turns, -ROUND, None, ALU.add))
                link(dve.scalar_tensor_tensor(red, turns, -TWO_PI_HI, ang, ALU.mult, ALU.add))
                link(dve.scalar_tensor_tensor(red, turns, -TWO_PI_LO, red, ALU.mult, ALU.add))
                link(dve.tensor_scalar(red, red, 3.1415925, -3.1415925, ALU.min, ALU.max))
                dve.wait_ge(setup_act, 3)
                link(dve.tensor_tensor(cos_t[:], cos_t[:], cos_t[:], ALU.mult))
                link(dve.tensor_scalar(cos_t[:], cos_t[:], -2.0, 1.0, ALU.mult, ALU.add))
                y, e, f = small[:, 6, 0:1], small[:, 6, 1:2], small[:, 6, 2:3]
                link(dve.tensor_tensor(y, small[:, 5, 0:1], small[:, 4, 0:1], ALU.mult))
                link(dve.tensor_scalar(y, y, 100.0, -1.0 / 256, ALU.min, ALU.mult))
                link(dve.memset(e, 1.0))
                for k in range(9, 1, -1):
                    link(dve.tensor_tensor(e, e, y, ALU.mult))
                    link(dve.tensor_scalar(e, e, 1.0 / k, 1.0, ALU.mult, ALU.add))
                link(dve.tensor_tensor(e, e, y, ALU.mult))
                for _ in range(8):
                    link(dve.tensor_scalar(f, e, 2.0, None, ALU.add))
                    link(dve.tensor_tensor(e, e, f, ALU.mult))
                link(dve.memset(rate[:], 1.0))
                link(dve.tensor_scalar(rate[:], rate[:], e, None, ALU.add))

            @block.scalar
            def _(act):
                act.wait_ge(loaded, 16 * n_loads)
                act.activation(small[:, 5, 0:1], small[:, 2, 0:1], ACT.Exp).then_inc(setup_act, 1)
                act.wait_ge(setup_step, 14)
                act.activation(sin_t[:], tT[:], ACT.Sin).then_inc(setup_act, 1)
                act.activation(cos_t[:], tT[:], ACT.Sin, scale=0.5).then_inc(setup_act, 1)

        def keys_shared(m, t):
            return m == 0 or t == 0

        def newton_rsqrt(dve, link, v, tmp1, y):
            link(dve.tensor_scalar(y.bitcast(I32), v.bitcast(I32), 1, None, ALU.logical_shift_right))
            link(dve.tensor_scalar(y.bitcast(I32), y.bitcast(I32), -1.0, RSQRT_MAGIC, ALU.mult, ALU.add))
            for _ in range(3):
                link(dve.tensor_tensor(tmp1, y, y, ALU.mult))
                link(dve.scalar_tensor_tensor(tmp1, tmp1, 0.5, v, ALU.mult, ALU.mult))
                link(dve.scalar_tensor_tensor(y, tmp1, -1.5, y, ALU.add, ALU.mult))

        def layer_norm(dve, link, dst, src):
            for t in range(TT):
                last = dve.bn_stats(stat[:, t, :], src[:, t, :])
            link(last)
            for t in range(TT):
                last = dve.bn_aggr(mv[:, t, :], stat[:, t, :])
            link(last)
            v, tmp1, y = small[:, 0, 0:TT], small[:, 1, 0:TT], small[:, 2, 0:TT]
            link(dve.tensor_scalar(v, mv[:, 0:TT, 1], EPS, None, ALU.add))
            newton_rsqrt(dve, link, v, tmp1, y)
            for t in range(TT):
                last = dve.tensor_scalar(dst[:, t, :], src[:, t, :], mv[:, t, 0:1], y[:, t:t + 1],
                                         ALU.subtract, ALU.mult)
            return last

        stages = [("ret", 0), ("att", 0), ("moe", 0), ("scan", 0), ("att", 1), ("moe", 1)]

        with nc.Fori(0, B) as b:
            with nc.Block() as block:

                @block.sync
                def _(sp):
                    sp.dma_start(x[:], a["x"][b].rearrange("(t p) c -> p t c", p=P)).then_inc(x_in, 16)
                    sp.wait_ge(x_done.sem, x_done.at(0, 1))
                    sp.dma_start(out[b].rearrange("(t p) c -> p t c", p=P), x[:]).then_inc(stored_it, 16)
                    sp.wait_ge(stored_it, 16)

                @block.gpsimd
                def _(pool):
                    for n in range(2):
                        pool.wait_ge(normed.sem, normed.at(1 + n, 1))
                        pool.tensor_tensor(h[:], z[:], b_o[:].unsqueeze(1).broadcast_to([P, TT, C]), ALU.add).then_inc(a_zb.sem, 1)
                        pool.wait_ge(a_h.sem, a_h.at(n, 1))
                        pool.tensor_tensor(x[:], x[:], h[:], ALU.add).then_inc(a_xh.sem, 1)

                @block.tensor
                def _(pe):
                    def transposes(dst, src, rows=P):
                        for t in range(TT):
                            last = pe.transpose(dst[0:rows, t * P:(t + 1) * P], src[:, t, :], ident[:])
                        return last

                    def front(m, w):
                        pe.wait_ge(normed.sem, normed.at(m, 1))
                        transposes(bank[0], (z if m == 0 else zn)).then_inc(normT.sem, 1)
                        pe.wait_ge(aT_ready.sem, aT_ready.at(m, 1))
                        for i in range(2):
                            pe.matmul(bank[1 + i][:], w[:, i, :], aT[:], start=True, stop=True).then_inc(qkv_ready.sem, 1)
                        for t in range(TT):
                            last = pe.matmul(bank[3][:, t * P:(t + 1) * P], aT[:, t * P:(t + 1) * P],
                                             w[:, 2, :], start=True, stop=True)
                        last.then_inc(qkv_ready.sem, 1)
                        pe.wait_ge(qk_split.sem, qk_split.at(m, 2))
                        spread_heads(m, 0)

                    def spread_heads(m, t):
                        if t >= 2:
                            heads_kept(m, t - 1)
                        for side in range(2):
                            dst = bank[SPREAD_BANKS[2 * (t % 2) + side]]
                            pe.matmul(dst[:], spread[:, 2 * side, t, :], qk_hi[:, side, :],
                                      start=True, stop=False)
                            pe.matmul(dst[:], spread[:, 2 * side + 1, t, :], qk_lo[:, side, :],
                                      start=False, stop=True).then_inc(spread_ready.sem, 1)

                    def heads_kept(m, n_groups):
                        pe.wait_ge(q_kept.sem, q_kept.at(m, n_groups))
                        pe.wait_ge(k_kept.sem, k_kept.at(m, n_groups))
                        pe.wait_ge(k_kept_v.sem, n_groups if m == 0 else NG + m)

                    def weighted_values(step, done, buf):
                        t, kt = step // TT, step % TT
                        for g in range(G):
                            last = pe.matmul(bank[X_BANKS[t % 2]][HR * g:HR * (g + 1), :],
                                             val[:, kt, G * t + g, :], probs[:, buf, g, :],
                                             start=(kt == 0), stop=(kt == TT - 1),
                                             tile_position=(0, HR * g))
                        last.then_inc(done.sem, 1)

                    def retention():
                        front(0, w_ret)

                        for t in range(1, NG):
                            spread_heads(0, t)
                        pe.wait_ge(v_ready.sem, v_ready.at(0, 1))
                        heads_kept(0, NG)

                        def head_scores(head):
                            t, g = head // G, head % G

                            def product(dst, kt, queries):
                                return pe.matmul(dst, Km[:, head, P * kt:P * (kt + 1)], Qs[:, t, queries],
                                                 start=True, stop=True)

                            dst = bank[R_BANKS[3 * (head % 2)]]
                            if head >= 2:
                                pe.wait_ge(r_diag.sem, r_diag.at(0, head - 1))
                            for kt in range(TT):
                                last = product(dst[:, P * kt:P * (kt + 1)], kt, slice(P * kt, P * (kt + 1)))
                            last.then_inc(r_scores.sem, 1)
                            if head >= 2:
                                pe.wait_ge(r_rest.sem, r_rest.at(0, 2 * head - 3))
                            product(bank[R_BANKS[3 * (head % 2) + 1]][:, 0:T - P], 0,
                                    slice(P, T)).then_inc(r_scores.sem, 1)
                            dst = bank[R_BANKS[3 * (head % 2) + 2]]
                            if head >= 2:
                                pe.wait_ge(r_rest.sem, r_rest.at(0, 2 * head - 2))
                            product(dst[:, 0:2 * P], 1, slice(2 * P, T))
                            product(dst[:, 2 * P:3 * P], 2, slice(3 * P, T)).then_inc(r_scores.sem, 1)

                        def sum_values(t, kt):
                            if kt == 0:
                                pe.wait_ge(r_diag.sem, r_diag.at(0, G * (t + 1)))
                                pe.wait_ge(r_rest.sem, r_rest.at(0, 2 * G * (t + 1)))
                                if t >= 2:
                                    pe.wait_ge(r_kept.sem, r_kept.at(0, t - 1))
                            behind = (0, T - P, T + P)[kt] if kt < TT - 1 else None
                            for g in range(G):
                                last = pe.matmul(bank[X_BANKS[t % 2]][HR * g:HR * (g + 1), P * kt:P * (kt + 1)],
                                                 val[:, kt, G * t + g, :], probs[:, t % 2, g, P * kt:P * (kt + 1)],
                                                 start=(kt == 0), stop=(kt in (0, TT - 1)),
                                                 tile_position=(0, HR * g))
                            if behind is not None:
                                for g in range(G):
                                    pe.matmul(bank[X_BANKS[t % 2]][HR * g:HR * (g + 1), P * (kt + 1):T],
                                              val[:, kt, G * t + g, :],
                                              r_behind[:, t % 2, g, behind:behind + T - P * (kt + 1)],
                                              start=(kt == 0), stop=False, tile_position=(0, HR * g))
                            else:
                                last.then_inc(r_summed.sem, 1)

                        for head in range(NH):
                            head_scores(head)
                            if head >= G:
                                sum_values(head // G - 1, head % G)
                        for kt in range(TT):
                            sum_values(NG - 1, kt)
                        pe.wait_ge(gn_local.sem, gn_local.at(0, 1))
                        pe.matmul(bank[0][:, 0:2 * NG], average[:],
                                             mv[:, 0:NG, :].rearrange("p t s -> p (t s)"),
                                             start=True, stop=True).then_inc(gn_mean.sem, 1)
                        pe.wait_ge(gn_local.sem, gn_local.at(0, 2))
                        pe.matmul(bank[1][:, 0:NG], average[:], gn[:, 2, :],
                                             start=True, stop=True).then_inc(gn_mean.sem, 1)
                        pe.wait_ge(gn_done.sem, gn_done.at(0, NG))
                        for tt in range(TT):
                            for t in range(NG):
                                last = pe.matmul(bank[2][:, P * tt:P * (tt + 1)],
                                                 head_out[:, t, P * tt:P * (tt + 1)], wo_ret[:, t, :],
                                                 start=(t == 0), stop=(t == NG - 1))
                        last.then_inc(r_out.sem, 1)

                    def attention(n):
                        front(1 + n, w_qkv)

                        def scores_for_max(head, qt):
                            i = head * TT + qt
                            if i >= 3:
                                pe.wait_ge(a_max.sem, a_max.at(n, i - 2))
                            pe.matmul(bank[MAX_BANKS[i % 3]][:], Qs[:, head // G, P * qt:P * (qt + 1)],
                                      Km[:, head, :], start=True, stop=True).then_inc(a_scores.sem, 1)

                        def queries_with_max(t):
                            pe.wait_ge(a_max.sem, a_max.at(n, G * TT * (t + 1)))
                            if t >= 2:
                                pe.wait_ge(a_kept.sem, a_kept.at(n, t - 1))
                                pe.wait_ge(a_ctx.sem, a_ctx.at(n, t - 1))
                            dst = bank[X_BANKS[t % 2]]
                            pe.matmul(dst[:], spread[:, 0, t, :], qk_hi[:, 0, :], start=True, stop=False)
                            pe.matmul(dst[:], spread[:, 1, t, :], qk_lo[:, 0, :], start=False, stop=False)
                            for qt in range(TT):
                                last = pe.matmul(dst[:, P * qt:P * (qt + 1)], neg_max[:, t % 2, qt, :],
                                                 ident_r[:], start=False, stop=(qt == TT - 1))
                            last.then_inc(a_qm.sem, 1)

                        def turn_out(t):
                            pe.wait_ge(a_kept.sem, a_kept.at(n, t + 1))
                            for qt in range(TT):
                                last = pe.transpose(bank[X_BANKS[t % 2]][:, P * qt:P * (qt + 1)],
                                                    head_out[:, t, P * qt:P * (qt + 1)], ident[:])
                            last.then_inc(a_outT.sem, 1)

                        def pv(step):
                            t, kt = step // TT, step % TT
                            pe.wait_ge(a_exp.sem, a_exp.at(n, G * (step + 1)))
                            if kt == 0:
                                pe.wait_ge(a_qm_kept.sem, a_qm_kept.at(n, t + 1))
                            weighted_values(step, a_pv, step % 2)

                        heads_kept(1 + n, 1)
                        for head in range(G):
                            if head + 1 < NG:
                                spread_heads(1 + n, head + 1)
                            for qt in range(TT):
                                scores_for_max(head, qt)
                        heads_kept(1 + n, NG)
                        pe.wait_ge(v_ready.sem, v_ready.at(1 + n, 1))
                        for head in range(G, LEAD):
                            for qt in range(TT):
                                scores_for_max(head, qt)
                        queries_with_max(0)
                        for step in range(NG * TT):
                            t, kt = step // TT, step % TT
                            if kt == 0:
                                pe.wait_ge(a_qm_kept.sem, a_qm_kept.at(n, t + 1))
                            for g in range(G):
                                i = step * G + g
                                if i >= 3:
                                    pe.wait_ge(a_exp.sem, a_exp.at(n, i - 2))
                                pe.matmul(bank[S_BANKS[i % 3]][:], Km[:, G * t + g, P * kt:P * (kt + 1)],
                                          Qs[:, t, :], start=True, stop=True).then_inc(a_scoresT.sem, 1)
                                if step + LEAD < NH:
                                    scores_for_max(step + LEAD, g)
                                if g == 1 and step:
                                    pv(step - 1)
                            if kt == 1 and t:
                                turn_out(t - 1)
                            if kt == TT - 1 and t + 1 < NG:
                                queries_with_max(t + 1)
                        pv(NG * TT - 1)
                        turn_out(NG - 1)
                        pe.wait_ge(a_ctx.sem, a_ctx.at(n, NG))
                        transposes(bank[0], ctxt).then_inc(a_ctxT.sem, 1)
                        pe.wait_ge(a_ctxT_kept.sem, a_ctxT_kept.at(n, 1))
                        for tt in range(TT):
                            last = pe.matmul(bank[1][:, P * tt:P * (tt + 1)], ctxT[:, P * tt:P * (tt + 1)],
                                             w_o[:], start=True, stop=True)
                        last.then_inc(a_proj.sem, 1)

                    def experts_stage(n):
                        pe.wait_ge(m_normed.sem, m_normed.at(n, 1))
                        transposes(bank[O_BANK], tn).then_inc(m_normT.sem, 1)
                        pe.wait_ge(m_tT.sem, m_tT.at(n, 1))
                        for tt in range(TT):
                            last = pe.matmul(bank[O_BANK][:, NE * tt:NE * (tt + 1)],
                                             tT[:, P * tt:P * (tt + 1)], w_gate[:], start=True, stop=True)
                        last.then_inc(m_logits.sem, 1)

                        def hidden(e):
                            for c in range(HC):
                                i = e * HC + c
                                if i >= 2:
                                    pe.wait_ge(m_gelu.sem, m_gelu.at(n, i - 1))
                                cols = slice(P * c, P * (c + 1))
                                dst = bank[6 + i % 2]
                                pe.matmul(dst[:], w1_hi[:, e, cols], t_hi[:], start=True, stop=False)
                                pe.matmul(dst[:], w1_hi[:, e, cols], t_lo[:], start=False, stop=False)
                                pe.matmul(dst[:], w1_lo[:, e, cols], t_hi[:],
                                                   start=False, stop=True).then_inc(m_hid.sem, 1)

                        def output(e):
                            pe.wait_ge(m_gelu.sem, m_gelu.at(n, HC * (e + 1)))
                            pe.wait_ge(m_acc.sem, m_acc.at(n, e + 1))
                            for tt in range(TT):
                                for c in range(HC):
                                    last = pe.matmul(bank[O_BANK][:, P * tt:P * (tt + 1)],
                                                     hid[:, e % 2, c, P * tt:P * (tt + 1)],
                                                     w2[:, e * HC + c, :], start=(c == 0), stop=(c == HC - 1))
                            last.then_inc(m_out.sem, 1)

                        pe.wait_ge(m_split.sem, m_split.at(n, 1))
                        hidden(0)
                        pe.wait_ge(m_we.sem, m_we.at(n, 1))
                        for tt in range(TT):
                            last = pe.transpose(bank[O_BANK][0:NE, P * tt:P * (tt + 1)], we[:, tt, :], ident[:])
                        last.then_inc(m_weT.sem, 1)
                        pe.wait_ge(m_weT_kept.sem, m_weT_kept.at(n, 1))
                        for tt in range(TT):
                            last = pe.matmul(bank[O_BANK][:, P * tt:P * (tt + 1)],
                                             weT[:, P * tt:P * (tt + 1)], b2[:], start=True, stop=True)
                        last.then_inc(m_bias.sem, 1)
                        for e in range(1, NE):
                            hidden(e)
                            output(e - 1)
                        output(NE - 1)

                    def scan():
                        pe.wait_ge(s_normed.sem, s_normed.at(0, 1))
                        transposes(bank[0], z).then_inc(s_normT.sem, 1)
                        pe.wait_ge(s_aT.sem, s_aT.at(0, 1))
                        pe.matmul(bank[3][:], w_sgate[:], aT[:], start=True, stop=True).then_inc(s_proj.sem, 1)
                        for i in range(2):
                            pe.matmul(bank[1 + i][:], w_psi[:, P * i:P * (i + 1)], aT[:],
                                                start=True, stop=True).then_inc(s_proj.sem, 1)
                        pe.wait_ge(s_u.sem, s_u.at(0, 2))
                        for tt in range(TT):
                            last = pe.matmul(bank[1 + tt // 2][:, 2 * P * (tt % 2):2 * P * (tt % 2 + 1)],
                                             aT[:, P * tt:P * (tt + 1)], w_phi[:], start=True, stop=True)
                        last.then_inc(s_phi.sem, 1)
                        for i in range(2):
                            pe.wait_ge(s_h.sem, s_h.at(0, i + 1))
                            for tt in range(TT):
                                last = pe.transpose(bank[3 + i][:, P * tt:P * (tt + 1)],
                                                    U[i][:, P * tt:P * (tt + 1)], ident[:])
                            last.then_inc(s_hT.sem, 1)

                    for kind, n in stages:
                        if kind == "ret":
                            retention()
                        elif kind == "att":
                            attention(n)
                        elif kind == "moe":
                            experts_stage(n)
                        else:
                            scan()

                @block.scalar
                def _(act):
                    def front(m):
                        act.wait_ge(normT.sem, normT.at(m, 1))
                        if m == 0:
                            act.copy(aT[:], bank[0][:]).then_inc(aT_ready.sem, 1)
                        else:
                            act.activation(aT[:], bank[0][:], ACT.Identity,
                                                       bias=ln_wb[:, 1:2], scale=ln_wb[:, 0:1]).then_inc(aT_ready.sem, 1)
                        for i in range(2):
                            if m:
                                act.wait_ge(qkv_ready.sem, qkv_ready.at(m, i + 1))
                                act.activation(qk_f[:, i, :], bank[1 + i][:], ACT.Identity,
                                               bias=b_qk[:, i:i + 1]).then_inc(qk_biased.sem, 1)
                        for t in range(NG):
                            act.wait_ge(spread_ready.sem, spread_ready.at(m, 2 * t + 1))
                            act.copy(Qs[:, t, :], bank[SPREAD_BANKS[2 * (t % 2)]][:]).then_inc(q_kept.sem, 1)
                            act.wait_ge(spread_ready.sem, spread_ready.at(m, 2 * t + 2))
                            for g in range(0, G // 2 if keys_shared(m, t) else G):
                                rows = slice(HR * g, HR * (g + 1))
                                last = act.activation(Km[rows, G * t + g, :],
                                                      bank[SPREAD_BANKS[2 * (t % 2) + 1]][rows, :],
                                                      ACT.Identity, bias=ones_row[rows, :])
                            last.then_inc(k_kept.sem, 1)

                    def retention():
                        front(0)
                        def keep(t):
                            act.wait_ge(r_summed.sem, r_summed.at(0, t + 1))
                            act.copy(head_out[:, t, :], bank[X_BANKS[t % 2]][:]).then_inc(r_kept.sem, 1)

                        for head in range(NH):
                            t, g = head // G, head % G
                            if g == 0 and t >= 2:
                                act.wait_ge(r_summed.sem, r_summed.at(0, t - 1))
                            for j in range(2):
                                act.wait_ge(r_scores.sem, r_scores.at(0, 3 * head + 2 + j))
                                act.copy(r_behind[:, t % 2, g, (T - P) * j:(T - P) * (j + 1)],
                                         bank[R_BANKS[3 * (head % 2) + 1 + j]][:, 0:T - P]).then_inc(r_rest.sem, 1)
                            if g == 1 and t >= 2:
                                keep(t - 2)
                        keep(NG - 2)
                        keep(NG - 1)
                        act.wait_ge(gn_coef.sem, gn_coef.at(0, 1))
                        for t in range(NG):
                            act.activation(head_out[:, t, :], head_out[:, t, :], ACT.Identity,
                                                      bias=gn[:, 5, t:t + 1], scale=gn[:, 4, t:t + 1]).then_inc(gn_done.sem, 1)

                    def attention(n):
                        front(1 + n)

                        def keep_queries(t):
                            act.wait_ge(a_qm.sem, a_qm.at(n, t + 1))
                            act.copy(Qs[:, t, :], bank[X_BANKS[t % 2]][:]).then_inc(a_qm_kept.sem, 1)

                        def keep_sums(t):
                            act.wait_ge(a_pv.sem, a_pv.at(n, TT * (t + 1)))
                            act.copy(head_out[:, t, :], bank[X_BANKS[t % 2]][:]).then_inc(a_kept.sem, 1)

                        keep_queries(0)
                        for step in range(NG * TT):
                            t, kt = step // TT, step % TT
                            for g in range(G):
                                i = step * G + g
                                act.wait_ge(a_scoresT.sem, a_scoresT.at(n, i + 1))
                                if g == 0 and step >= 2:
                                    act.wait_ge(a_pv.sem, a_pv.at(n, step - 1))
                                act.activation(probs[:, step % 2, g, :], bank[S_BANKS[i % 3]][:],
                                               ACT.Exp, scale=SCALE).then_inc(a_exp.sem, 1)
                            if kt == 0 and t:
                                keep_sums(t - 1)
                            if kt == TT - 1 and t + 1 < NG:
                                keep_queries(t + 1)
                        keep_sums(NG - 1)
                        act.wait_ge(a_ctxT.sem, a_ctxT.at(n, 1))
                        act.copy(ctxT[:], bank[0][:]).then_inc(a_ctxT_kept.sem, 1)

                    def experts_stage(n):
                        act.wait_ge(m_normT.sem, m_normT.at(n, 1))
                        act.activation(tT[:], bank[O_BANK][:], ACT.Identity,
                                               bias=ln_wb[:, 3:4], scale=ln_wb[:, 2:3]).then_inc(m_tT.sem, 1)
                        act.wait_ge(m_gap.sem, m_gap.at(n, 1))
                        act.activation(gw[:, 1, :], gw[:, 0, :], ACT.Exp).then_inc(m_gap_exp.sem, 1)
                        for e in range(NE):
                            for c in range(HC):
                                i = e * HC + c
                                act.wait_ge(m_hid.sem, m_hid.at(n, i + 1))
                                if c == 0 and e >= 2:
                                    act.wait_ge(m_out.sem, m_out.at(n, e - 1))
                                act.activation(hid[:, e % 2, c, :], bank[6 + i % 2][:],
                                                         ACT.Gelu_apprx_tanh, bias=b1[:, i:i + 1]).then_inc(m_gelu.sem, 1)

                    def scan():
                        act.wait_ge(s_normT.sem, s_normT.at(0, 1))
                        act.copy(aT[:], bank[0][:]).then_inc(s_aT.sem, 1)
                        act.wait_ge(s_proj.sem, s_proj.at(0, 1))
                        act.activation(sig, bank[3][:], ACT.Exp, bias=nb_sgate[:], scale=-1.0).then_inc(s_gexp.sem, 1)

                    for kind, n in stages:
                        if kind == "ret":
                            retention()
                        elif kind == "att":
                            attention(n)
                        elif kind == "moe":
                            experts_stage(n)
                        else:
                            scan()

                @block.vector
                def _(dve):
                    steps = [0]

                    def link(ins):
                        steps[0] += 1
                        ins.then_inc(vec_step, 1)
                        dve.wait_ge(vec_step, steps[0])

                    def front(m):
                        if m == 0:
                            dve.wait_ge(x_in, 16)
                            layer_norm(dve, link, z, x).then_inc(normed.sem, 1)
                        else:
                            link(layer_norm(dve, link, z, x))
                            layer_norm(dve, link, zn, z).then_inc(normed.sem, 1)
                        for i in range(2):
                            if m == 0:
                                dve.wait_ge(qkv_ready.sem, qkv_ready.at(m, i + 1))
                                link(dve.tensor_tensor(qk_f[:, i, :], bank[1 + i][:], qk_decay[:, i, :], ALU.mult))
                            else:
                                dve.wait_ge(qk_biased.sem, qk_biased.at(m - 1, i + 1))
                            link(dve.tensor_copy(qk_hi[:, i, :], qk_f[:, i, :]))
                            dve.tensor_tensor(qk_lo[:, i, :], qk_f[:, i, :], qk_hi[:, i, :].bitcast(F32),
                                              ALU.subtract).then_inc(qk_split.sem, 1)
                        dve.wait_ge(qkv_ready.sem, qkv_ready.at(m, 3))
                        src = bank[3][:].rearrange("p (t h d) -> p t h d", t=TT, h=NH)
                        if m == 0:
                            dve.tensor_copy(val[:, :, :, 0:DH], src).then_inc(v_ready.sem, 1)
                        else:
                            dve.tensor_tensor(val[:, :, :, 0:DH], src,
                                                         b_v[:].rearrange("p (h d) -> p h d", h=NH).unsqueeze(1).broadcast_to([P, TT, NH, DH]), ALU.add).then_inc(v_ready.sem, 1)
                        keep_keys(m, 0)

                    def keep_keys(m, t):
                        dve.wait_ge(spread_ready.sem, spread_ready.at(m, 2 * t + 2))
                        for g in range(G // 2, G):
                            rows = slice(HR * g, HR * (g + 1))
                            last = dve.tensor_scalar(Km[rows, G * t + g, :],
                                                     bank[SPREAD_BANKS[2 * (t % 2) + 1]][rows, :],
                                                     ones_row[rows, :], None, ALU.add)
                        last.then_inc(k_kept_v.sem, 1)

                    def retention():
                        front(0)
                        for t in range(1, NG):
                            keep_keys(0, t)
                        for head in range(NH):
                            t, g = head // G, head % G
                            if g == 0 and t >= 2:
                                dve.wait_ge(r_summed.sem, r_summed.at(0, t - 1))
                            dve.wait_ge(r_scores.sem, r_scores.at(0, 3 * head + 1))
                            dve.tensor_tensor(probs[:, t % 2, g, :].rearrange("p (k q) -> p k q", k=TT),
                                              bank[R_BANKS[3 * (head % 2)]][:].rearrange("p (k q) -> p k q", k=TT),
                                              causal[:].unsqueeze(1).broadcast_to([P, TT, P]),
                                              ALU.mult).then_inc(r_diag.sem, 1)
                            if g == 2 and t >= 2:
                                dve.wait_ge(r_kept.sem, r_kept.at(0, t - 1))
                                dve.bn_stats(stat[:, t - 2, :], head_out[:, t - 2, :])
                        dve.wait_ge(r_kept.sem, r_kept.at(0, NG - 1))
                        dve.bn_stats(stat[:, NG - 2, :], head_out[:, NG - 2, :])
                        dve.wait_ge(r_kept.sem, r_kept.at(0, NG))
                        link(dve.bn_stats(stat[:, NG - 1, :], head_out[:, NG - 1, :]))
                        for t in range(NG):
                            last = dve.bn_aggr(mv[:, t, :], stat[:, t, :])
                        last.then_inc(gn_local.sem, 1)
                        dve.wait_ge(gn_mean.sem, gn_mean.at(0, 1))
                        avg = bank[0][:, 0:2 * NG].rearrange("p (t s) -> p s t", s=2)
                        link(dve.tensor_copy(gn[:, 0:2, :], avg))
                        gn_local_done = dve.tensor_tensor(gn[:, 2, :], mv[:, 0:NG, 0], gn[:, 0, :], ALU.subtract)
                        link(gn_local_done)
                        dve.tensor_tensor(gn[:, 2, :], gn[:, 2, :], gn[:, 2, :], ALU.mult).then_inc(gn_local.sem, 1)
                        dve.wait_ge(gn_mean.sem, gn_mean.at(0, 2))
                        v = small[:, 0, 0:NG]
                        link(dve.scalar_tensor_tensor(v, gn[:, 1, :], EPS, bank[1][:, 0:NG], ALU.add, ALU.add))
                        newton_rsqrt(dve, link, v, small[:, 1, 0:NG], gn[:, 3, :])
                        link(dve.tensor_tensor(gn[:, 4, :], gn[:, 3, :], gn_w[:], ALU.mult))
                        link(dve.tensor_tensor(small[:, 0, 0:NG], gn[:, 0, :], gn[:, 4, :], ALU.mult))
                        dve.tensor_tensor(gn[:, 5, :], gn_b[:], small[:, 0, 0:NG], ALU.subtract).then_inc(gn_coef.sem, 1)
                        dve.wait_ge(r_out.sem, r_out.at(0, 1))
                        xf = x[:].rearrange("p t c -> p (t c)")
                        link(dve.tensor_tensor(xf, bank[2][:], xf, ALU.add))

                    def attention(n):
                        front(1 + n)

                        def maxima(head):
                            t, g = head // G, head % G
                            if g == 0 and t >= 2:
                                dve.wait_ge(a_qm.sem, a_qm.at(n, t - 1))
                            for qt in range(TT):
                                i = head * TT + qt
                                dve.wait_ge(a_scores.sem, a_scores.at(n, i + 1))
                                col = HR * g + MAX_ROW
                                dve.tensor_reduce(neg_max[:, t % 2, qt, col:col + 1], bank[MAX_BANKS[i % 3]][:],
                                                  AX_X, ALU.max, negate=True).then_inc(a_max.sem, 1)

                        def normalise(t):
                            dve.wait_ge(a_outT.sem, a_outT.at(n, t + 1))
                            if t:
                                dve.wait_ge(a_ctx.sem, a_ctx.at(n, t))
                            else:
                                dve.wait_ge(a_zb.sem, a_zb.at(n, 1))
                            src = bank[X_BANKS[t % 2]][:].rearrange("p (q g r) -> p q g r", q=TT, g=G)
                            link(dve.reciprocal(rden[:], src[:, :, :, DEN]))
                            dst = ctxt[:, :, C // NG * t:C // NG * (t + 1)].rearrange("p q (g d) -> p q g d", g=G)
                            dve.tensor_tensor(dst, src[:, :, :, 0:DH],
                                              rden[:].unsqueeze(3).broadcast_to([P, TT, G, DH]),
                                              ALU.mult).then_inc(a_ctx.sem, 1)

                        for head in range(LEAD):
                            maxima(head)
                        for step in range(NG * TT):
                            t, kt = step // TT, step % TT
                            if step + LEAD < NH:
                                maxima(step + LEAD)
                            if kt == 1 and t:
                                normalise(t - 1)
                        normalise(NG - 1)
                        dve.wait_ge(a_proj.sem, a_proj.at(n, 1))
                        dve.wait_ge(a_zb.sem, a_zb.at(n, 1))
                        dve.tensor_tensor(h[:].rearrange("p t c -> p (t c)"), bank[1][:],
                                                 h[:].rearrange("p t c -> p (t c)"), ALU.add).then_inc(a_h.sem, 1)
                        dve.wait_ge(a_h.sem, a_h.at(n, 1))

                    def experts_stage(n):
                        layer_norm(dve, link, tn, h).then_inc(m_normed.sem, 1)
                        dve.wait_ge(m_tT.sem, m_tT.at(n, 1))
                        link(dve.tensor_copy(t_hi[:], tT[:]))
                        dve.tensor_tensor(t_lo[:], tT[:], t_hi[:].bitcast(F32), ALU.subtract).then_inc(m_split.sem, 1)
                        dve.wait_ge(m_logits.sem, m_logits.at(n, 1))
                        link(dve.tensor_copy(logits[:].rearrange("p t e -> p (t e)"), bank[O_BANK][:, 0:TT * NE]))
                        for t in range(TT):
                            last = dve.max(top[:, t, :], logits[:, t, :])
                        link(last)
                        for t in range(TT):
                            last = dve.max_index(top_i[:, t, :], top[:, t, :], logits[:, t, :])
                        dve.tensor_tensor(gw[:, 0, :], top[:, :, 1], top[:, :, 0], ALU.subtract).then_inc(m_gap.sem, 1)
                        dve.wait_ge(m_gap.sem, m_gap.at(n, 1))
                        link(dve.tensor_copy(top_f[:], top_i[:]))
                        for k in range(2):
                            last = dve.tensor_tensor(hot[:, k], experts[:],
                                                     top_f[:, :, k:k + 1].broadcast_to([P, TT, NE]), ALU.is_equal)
                        dve.wait_ge(m_gap_exp.sem, m_gap_exp.at(n, 1))
                        link(last)
                        link(dve.tensor_scalar(gw[:, 2, :], gw[:, 1, :], 1.0, None, ALU.add))
                        link(dve.reciprocal(gw[:, 2, :], gw[:, 2, :]))
                        link(dve.tensor_tensor(gw[:, 3, :], gw[:, 1, :], gw[:, 2, :], ALU.mult))
                        for k in range(2):
                            last = dve.tensor_tensor(hot[:, k], hot[:, k],
                                                     gw[:, 2 + k, :].unsqueeze(2).broadcast_to([P, TT, NE]), ALU.mult)
                        link(last)
                        dve.tensor_tensor(we[:], hot[:, 0], hot[:, 1], ALU.add).then_inc(m_we.sem, 1)
                        dve.wait_ge(m_weT.sem, m_weT.at(n, 1))
                        dve.tensor_copy(weT[:], bank[O_BANK][0:NE, :]).then_inc(m_weT_kept.sem, 1)
                        dve.wait_ge(m_bias.sem, m_bias.at(n, 1))
                        dve.wait_ge(a_xh.sem, a_xh.at(n, 1))
                        dve.tensor_tensor(x[:].rearrange("p t c -> p (t c)"), bank[O_BANK][:],
                                                   x[:].rearrange("p t c -> p (t c)"), ALU.add).then_inc(m_acc.sem, 1)
                        for e in range(NE):
                            dve.wait_ge(m_out.sem, m_out.at(n, e + 1))
                            dve.wait_ge(m_acc.sem, m_acc.at(n, e + 1))
                            for t in range(TT):
                                last = dve.scalar_tensor_tensor(x[:, t, :], bank[O_BANK][:, P * t:P * (t + 1)],
                                                                we[:, t, e:e + 1], x[:, t, :], ALU.mult, ALU.add)
                            last.then_inc(m_acc.sem, 1)
                        dve.wait_ge(m_acc.sem, m_acc.at(n, NE + 1))
                        if n == 1:
                            dve.tensor_copy(small[:, 7, 0:1], x[:, 0, 0:1]).then_inc(x_done.sem, 1)

                    def scan():
                        layer_norm(dve, link, z, x).then_inc(s_normed.sem, 1)
                        dve.wait_ge(s_gexp.sem, s_gexp.at(0, 1))
                        link(dve.tensor_scalar(sig, sig, 1.0, None, ALU.add))
                        link(dve.reciprocal(sig, sig))
                        for i in range(2):
                            dve.wait_ge(s_proj.sem, s_proj.at(0, 2 + i))
                            dve.scalar_tensor_tensor(U[i], bank[1 + i][:], b_psi[:, i:i + 1], sig,
                                                            ALU.add, ALU.mult).then_inc(s_u.sem, 1)
                        dve.wait_ge(s_u.sem, s_u.at(0, 2))
                        dve.tensor_tensor(tmp[0], U[0], cos_t[:], ALU.mult)
                        dve.tensor_tensor(tmp[1], U[1], sin_t[:], ALU.mult)
                        dve.tensor_tensor(W[0], U[1], cos_t[:], ALU.mult)
                        link(dve.tensor_tensor(W[1], U[0], sin_t[:], ALU.mult))
                        dve.tensor_tensor(rot[0], tmp[0], tmp[1], ALU.add)
                        link(dve.tensor_tensor(rot[1], W[0], W[1], ALU.subtract))
                        dve.tensor_tensor_scan(W[0], rate[:].broadcast_to([P, T]), rot[0], 0.0, ALU.mult, ALU.add)
                        link(dve.tensor_tensor_scan(W[1], rate[:].broadcast_to([P, T]), rot[1], 0.0, ALU.mult, ALU.add))
                        dve.tensor_tensor(tmp[0], W[0], cos_t[:], ALU.mult)
                        dve.tensor_tensor(tmp[1], W[1], sin_t[:], ALU.mult)
                        dve.tensor_tensor(rot[0], W[0], sin_t[:], ALU.mult)
                        link(dve.tensor_tensor(rot[1], W[1], cos_t[:], ALU.mult))
                        dve.tensor_tensor(U[0], tmp[0], tmp[1], ALU.subtract).then_inc(s_h.sem, 1)
                        dve.tensor_tensor(U[1], rot[0], rot[1], ALU.add).then_inc(s_h.sem, 1)
                        dve.wait_ge(s_phi.sem, s_phi.at(0, 1))
                        for i in range(2):
                            last = dve.tensor_tensor(phi[:, 2 * i:2 * i + 2, :],
                                                     bank[1 + i][:].rearrange("p (t e) -> p t e", t=2),
                                                     b_phi[:].unsqueeze(1).broadcast_to([P, 2, 2 * P]), ALU.add)
                        dve.wait_ge(s_hT.sem, s_hT.at(0, 2))
                        link(last)
                        for i in range(2):
                            for t in range(TT):
                                last = dve.bn_stats(stat[:, TT * i + t, :], bank[3 + i][:, P * t:P * (t + 1)])
                        link(last)
                        for j in range(2 * TT):
                            last = dve.bn_aggr(mv[:, j, :], stat[:, j, :])
                        link(last)
                        v, t1, y = small[:, 0, :], small[:, 1, :], small[:, 2, :]
                        link(dve.tensor_scalar(v, mv[:, :, 1], TINY, None, ALU.add))
                        newton_rsqrt(dve, link, v, t1, y)
                        link(dve.tensor_tensor(y, y, mv[:, :, 1], ALU.mult))
                        link(dve.tensor_scalar(y, y, PROJ_EPS, None, ALU.add))
                        link(dve.reciprocal(y, y))
                        for i in range(2):
                            for t in range(TT):
                                j = TT * i + t
                                last = dve.tensor_scalar(Hn[:, i, t, :], bank[3 + i][:, P * t:P * (t + 1)],
                                                         mv[:, j, 0:1], y[:, j:j + 1], ALU.subtract, ALU.mult)
                        link(last)
                        for i in range(2):
                            last = dve.tensor_tensor(Hn[:, i], Hn[:, i], phi[:, :, P * i:P * (i + 1)], ALU.mult)
                        link(last)
                        link(dve.tensor_tensor(Hn[:, 0], Hn[:, 0], Hn[:, 1], ALU.add))
                        link(dve.tensor_tensor(x[:], x[:], Hn[:, 0], ALU.add))

                    for kind, n in stages:
                        if kind == "ret":
                            retention()
                        elif kind == "att":
                            attention(n)
                        elif kind == "moe":
                            experts_stage(n)
                        else:
                            scan()

            nums = sorted(s.num for s in sems)
            assert nums == list(range(nums[0], nums[-1] + 1))
            nc.all_engine_barrier(sems_to_clear=range(nums[0], nums[-1] + 1))


_TRANSPOSED = ("L0_attn_a_wq", "L0_attn_a_wk", "L0_attn_a_wv", "L0_attn_a_wo",
               "L0_attn_b_W_psi", "L0_attn_b_W_phi", "L0_attn_b_W_gate")


def kernel(**inputs):
    import concourse.bacc as _bacc
    from concourse.bass_utils import run_bass_kernel_spmd as _run

    nc = _bacc.Bacc("TRN2", target_bir_lowering=False, num_devices=1)
    arrays = {}
    for name, v in inputs.items():
        v = np.asarray(v)
        if name == "L0_attn_a_x":
            name = "x"
        if name in _TRANSPOSED:
            v = v.T
        if name in ("L0_ffn_b1", "L0_attn_b_b_psi"):
            v = v.reshape(-1, P).T
        if name in ("L0_attn_a_gn_w", "L0_attn_a_gn_b"):
            v = v.reshape(NG, G, DH).transpose(1, 2, 0)
        if v.ndim == 0:
            v = v.reshape(1)
        arrays[name] = np.ascontiguousarray(v)
    arrays.update(shape_constants())
    aps = {name: nc.dram_tensor("in_" + name, v.shape, F32, kind="ExternalInput").ap()
           for name, v in arrays.items()}
    out = nc.dram_tensor("out", (B, T, C), F32, kind="ExternalOutput").ap()
    build(nc, aps, out)
    r = _run(nc, [{"in_" + name: v for name, v in arrays.items()}], core_ids=[0])
    return r.results[0]["out"]
```

```python
from contextlib import ExitStack

import numpy as np

import concourse.bass as bass
from concourse import mybir

F32 = mybir.dt.float32
F32R = mybir.dt.float32r
I32 = mybir.dt.int32
U32 = mybir.dt.uint32
ALU = mybir.AluOpType
ACT = mybir.ActivationFunctionType
AX_X = mybir.AxisListType.X

B, T, C = 16, 512, 128
P = 128
TT = T // P
NH = 16
DH = C // NH
G = 4
NG = NH // G
HR = P // G
MAX_ROW = 3 * DH
DEN = DH
NE, NHID = 8, 512
HC = NHID // P
EPS = 1e-5
PROJ_EPS = 1e-6
TINY = 1e-30
SCALE = float(1.0 / np.sqrt(np.float32(DH)))
Q_TERMS = (0, 0, 1)
K_TERMS = (0, 1, 0)
RSQRT_MAGIC = float(0x5F3759DF - (1 << 31))
TWO_PI_HI = 6.28125
TWO_PI_LO = float(2 * np.pi - 6.28125)
ROUND = 12582912.0
REST = P * TT * (TT - 1) // 2
LEAD = 5


def shape_constants():
    lo, hi = np.log(np.float32(1.0 - 0.999)), np.log(np.float32(1.0 - 0.9))
    gammas = (1.0 - np.exp(np.linspace(float(lo), float(hi), NH).astype(np.float32))).astype(np.float32)
    pos = np.arange(T, dtype=np.float64)
    g64 = gammas.astype(np.float64)
    q_decay = np.repeat(g64, DH)[:, None] ** pos
    k_decay = np.repeat(g64, DH)[:, None] ** -pos
    causal = (np.arange(P)[None, :] >= np.arange(P)[:, None])
    spread = np.zeros((P, 4, NG, P), np.float32)
    average = np.zeros((P, P), np.float32)
    ones_row = np.zeros((P, 1), np.float32)
    for t in range(NG):
        for g in range(G):
            for d in range(DH):
                for term in range(3):
                    spread[(G * t + g) * DH + d, Q_TERMS[term], t, HR * g + DH * term + d] = 1.0
                    spread[(G * t + g) * DH + d, 2 + K_TERMS[term], t, HR * g + DH * term + d] = 1.0
    for g in range(G):
        average[HR * g:HR * g + DH, HR * g:HR * g + DH] = 1.0 / DH
        ones_row[HR * g + MAX_ROW] = 1.0
    return {
        "c_q_decay": q_decay.astype(np.float32),
        "c_k_decay": k_decay.astype(np.float32),
        "c_causal": causal.astype(np.float32),
        "c_spread": spread.reshape(P, 4 * NG * P),
        "c_average": average,
        "c_ones_row": ones_row,
        "c_identity": np.eye(P, dtype=np.float32),
        "c_experts": np.tile(np.arange(NE, dtype=np.float32), (P, TT)),
        "c_time": np.tile(np.arange(T, dtype=np.float32), (P, 1)),
    }


class Signal:

    def __init__(self, sem, per):
        self.sem, self.per = sem, per

    def at(self, run, k):
        return run * self.per + k


def build(nc, a, out):
    with ExitStack() as ctx:
        def sb(name, shape, dt=F32):
            return ctx.enter_context(nc.sbuf_tensor(name, shape, dt))

        ident = sb("ident", [P, P])
        ident_r = sb("ident_r", [P, P], F32R)
        qk_decay = sb("qk_decay", [P, 2, T])
        causal = sb("causal", [P, P])
        spread = sb("spread", [P, 4, NG, P], F32R)
        average = sb("average", [P, P])
        ones_row = sb("ones_row", [P, 1])
        experts = sb("experts", [P, TT, NE])
        w_ret = sb("w_ret", [P, 3, P])
        wo_ret = sb("wo_ret", [P, NG, P])
        gn_w = sb("gn_w", [P, NG])
        gn_b = sb("gn_b", [P, NG])
        w_qkv = sb("w_qkv", [P, 3, P])
        b_qk = sb("b_qk", [P, 2])
        b_v = sb("b_v", [P, P])
        b_o = sb("b_o", [P, P])
        w_o = sb("w_o", [P, P])
        ln_wb = sb("ln_wb", [P, 4])
        w_gate = sb("w_gate", [P, NE])
        w1_hi = sb("w1_hi", [P, NE, NHID], F32R)
        w1_lo = sb("w1_lo", [P, NE, NHID], F32R)
        b1 = sb("b1", [P, NE * HC])
        w2 = sb("w2", [P, NE * HC, P])
        b2 = sb("b2", [NE, P])
        w_psi = sb("w_psi", [P, 2 * P])
        w_sgate = sb("w_sgate", [P, P])
        w_phi = sb("w_phi", [P, 2 * P])
        b_psi = sb("b_psi", [P, 2])
        nb_sgate = sb("nb_sgate", [P, 1])
        b_phi = sb("b_phi", [P, 2 * P])
        cos_t = sb("cos_t", [P, T])
        sin_t = sb("sin_t", [P, T])
        rate = sb("rate", [P, 1])

        x = sb("x", [P, 2, TT, C])
        z = sb("z", [P, TT, C])
        h = sb("h", [P, 2, TT, C])
        aT = sb("aT", [P, T])
        with nc.sbuf_tensor("qk_hi", [P, 2, T], F32R) as qk_hi, nc.sbuf_tensor("qk_lo", [P, 2, T], F32R) as qk_lo:
            pass
        r_behind = sb("r_behind", [P, 2, G, REST])
        spare = r_behind[:].rearrange("p a g q -> p (a g q)")
        val = sb("val", [P, TT * NH * (DH + 1) + HR])
        val_heads = val[:, 0:TT * NH * (DH + 1)].rearrange("p (t h r) -> p t h r", t=TT, h=NH)
        Qs = sb("Qs", [P, NG, T], F32R)
        Km = sb("Km", [P, NH, T], F32R)
        neg_max = sb("neg_max", [P, 2, TT, P], F32R)
        probs = sb("probs", [P, 2, G, T])
        head_out = sb("head_out", [P, NG, T])
        qk_f = head_out[:, 0:2, :]
        rden = sb("rden", [P, TT, G])
        ctxt = z
        ctxT = aT
        stat = sb("stat", [P, 8, 6])
        mv = sb("mv", [P, 8, 2])
        small = sb("small", [P, 8, 8])
        gn = sb("gn", [P, 6, NG])
        zn = probs[:, 0, 0, :].rearrange("p (t c) -> p t c", t=TT)
        hid = sb("hid", [P, 2, HC, T])
        tn = hid[:, 1, 2, :].rearrange("p (t c) -> p t c", t=TT)
        tT = hid[:, 1, 3, :]
        m_stat = sb("m_stat", [P, TT, 6])
        m_mv = sb("m_mv", [P, TT, 2])
        m_small = sb("m_small", [P, 3, TT])
        t_hi = sb("t_hi", [P, T], F32R)
        t_lo = sb("t_lo", [P, T], F32R)
        logits = sb("logits", [P, TT, NE])
        top = sb("top", [P, TT, 8])
        top_i = sb("top_i", [P, TT, 8], U32)
        top_f = sb("top_f", [P, TT, 8])
        gw = sb("gw", [P, 4, TT])
        hot = sb("hot", [P, 2, TT, NE])
        we = sb("we", [P, TT, NE])
        weT = sb("weT", [NE, T])
        def spare_tile(k):
            return spare[:, k * T:(k + 1) * T]

        z_next = spare_tile(REST * 2 * G // T - 1).rearrange("p (t c) -> p t c", t=TT)
        U = [spare_tile(i) for i in range(2)]
        rot = [spare_tile(2 + i) for i in range(2)]
        tmp = [spare_tile(4 + i) for i in range(2)]
        W = [spare_tile(6 + i) for i in range(2)]
        sig = qk_f[:, 0, :]
        phi = probs[:, 0, 0:2, :].rearrange("p a t -> p (a t)").rearrange("p (t e) -> p t e", t=TT)
        Hn = probs[:, 1, 0:2, :].rearrange("p a (t c) -> p a t c", t=TT)

        bank = [ctx.enter_context(nc.psum_tensor(f"bank{i}", [P, T], F32)) for i in range(8)]
        MAX_BANKS = (0, 1, 6)
        S_BANKS = (2, 3, 5)
        X_BANK = 4
        QM_BANK = TURN_BANK = 7
        R_BANKS = 4
        O_BANK, H_BANK = 5, 6

        sems = []

        def sem(name):
            s = ctx.enter_context(nc.semaphore(name))
            return s

        loaded = sem("loaded")
        setup_step = sem("setup_step")
        setup_act = sem("setup_act")
        signals = {}

        def signal(name, per):
            s = sem(name)
            sems.append(s)
            signals[name] = Signal(s, per)
            return signals[name]

        x_in = [sem("x_in"), sem("x1_in")]
        sems.extend(x_in)
        stored_it = sem("stored_it")
        sems.append(stored_it)
        vec_step = sem("vec_step")
        sems.append(vec_step)
        normed = signal("normed", 1)
        normT = signal("normT", 1)
        aT_ready = signal("aT_ready", 1)
        qkv_ready = signal("qkv_ready", 3)
        qk_biased = signal("qk_biased", 2)
        q_hi = signal("q_hi", 1)
        q_split = signal("q_split", 1)
        k_split = signal("k_split", 1)
        v_ready = signal("v_ready", 1)
        spread_ready = signal("spread_ready", 8)
        q_kept = signal("q_kept", NG)
        k_kept = signal("k_kept", NG)
        k_kept_v = signal("k_kept_v", 0)
        r_scores = signal("r_scores", 3 * NH)
        r_diag = signal("r_diag", NH)
        r_rest = signal("r_rest", 2 * NH)
        r_summed = signal("r_summed", NG)
        r_kept = signal("r_kept", NG)
        gn_local = signal("gn_local", 2)
        gn_mean = signal("gn_mean", 2)
        gn_done = signal("gn_done", NG)
        r_out = signal("r_out", 1)
        a_scores = signal("a_scores", NH * TT)
        a_max = signal("a_max", NH * TT)
        a_qm = signal("a_qm", NG)
        a_qm_kept = signal("a_qm_kept", NG)
        a_scoresT = signal("a_scoresT", NH * TT)
        a_exp = signal("a_exp", NH * TT)
        a_pv = signal("a_pv", NG * TT)
        a_kept = signal("a_kept", NG)
        a_outT = signal("a_outT", NG)
        a_ctx = signal("a_ctx", NG)
        a_ctxT = signal("a_ctxT", 1)
        a_ctxT_kept = signal("a_ctxT_kept", 1)
        a_proj = signal("a_proj", 1)
        a_z = signal("a_z", 1)
        a_zb = signal("a_zb", 1)
        a_h = signal("a_h", 1)
        a_xh = signal("a_xh", 1)
        m_normed = signal("m_normed", 1)
        m_normT = signal("m_normT", 1)
        m_tT = signal("m_tT", 1)
        m_hi = signal("m_hi", 1)
        m_split = signal("m_split", 1)
        m_logits = signal("m_logits", 1)
        m_gap = signal("m_gap", 1)
        m_gap_exp = signal("m_gap_exp", 1)
        m_we = signal("m_we", 1)
        m_weT = signal("m_weT", 1)
        m_weT_kept = signal("m_weT_kept", 1)
        m_bias = signal("m_bias", 1)
        m_hid = signal("m_hid", NE * HC)
        m_gelu = signal("m_gelu", NE * HC)
        m_out = signal("m_out", NE)
        m_acc = signal("m_acc", NE + 1)
        s_normed = signal("s_normed", 1)
        s_normT = signal("s_normT", 1)
        s_aT = signal("s_aT", 1)
        s_proj = signal("s_proj", 3)
        s_gexp = signal("s_gexp", 1)
        s_u = signal("s_u", 2)
        s_phi = signal("s_phi", 1)
        s_h = signal("s_h", 2)
        s_hT = signal("s_hT", 2)

        with nc.Block() as block:
            loads = []

            @block.sync
            def _(sp):
                def load(dst, src):
                    loads.append(1)
                    sp.dma_start(dst, src).then_inc(loaded, 16)

                load(ident[:], a["c_identity"])
                load(hid[:, 0, :, :].rearrange("p c t -> p (c t)"), a["c_spread"])
                load(probs[:, :, :, :].rearrange("p a g t -> p (a g) t")[:, 0:NE, :],
                     a["L0_ffn_w1"].rearrange("e d h -> d e h"))
                load(qk_decay[:, 0, :], a["c_q_decay"])
                load(qk_decay[:, 1, :], a["c_k_decay"])
                load(causal[:], a["c_causal"])
                load(average[:], a["c_average"])
                load(ones_row[:], a["c_ones_row"])
                load(experts[:].rearrange("p t e -> p (t e)"), a["c_experts"])
                load(h[:, 0].rearrange("p t c -> p (t c)"), a["c_time"])
                for i, n in enumerate(("wq", "wk", "wv")):
                    load(w_ret[:, i, :], a["L0_attn_a_" + n])
                load(w_qkv[:].rearrange("p a n -> p (a n)"), a["L0_ffn_w_qkv"])
                for i in range(2):
                    load(b_qk[:, i:i + 1], a["L0_ffn_b_qkv"][C * i:C * (i + 1)].rearrange("(p o) -> p o", o=1))
                load(b_v[:], a["L0_ffn_b_qkv"][2 * C:3 * C].partition_broadcast(P))
                load(b_o[:], a["L0_ffn_b_o"].partition_broadcast(P))
                load(b_phi[:], a["L0_attn_b_b_phi"].partition_broadcast(P))
                load(w_o[:], a["L0_ffn_w_o"])
                for i, n in enumerate(("ln1_w", "ln1_b", "ln2_w", "ln2_b")):
                    load(ln_wb[:, i:i + 1], a["L0_ffn_" + n].rearrange("(p o) -> p o", o=1))
                load(w_gate[:], a["L0_ffn_w_gate"])
                load(b1[:], a["L0_ffn_b1"])
                load(w2[:], a["L0_ffn_w2"].rearrange("e (c p) n -> p (e c) n", p=P))
                load(b2[:], a["L0_ffn_b2"])
                load(w_psi[:], a["L0_attn_b_W_psi"])
                load(w_sgate[:], a["L0_attn_b_W_gate"])
                load(w_phi[:], a["L0_attn_b_W_phi"])
                load(b_psi[:], a["L0_attn_b_b_psi"])
                load(small[:, 0, 0:1], a["L0_attn_b_b_gate"].rearrange("(p o) -> p o", o=1))
                load(small[:, 1, 0:1], a["L0_attn_b_omega"].rearrange("(p o) -> p o", o=1))
                load(small[:, 2, 0:1], a["L0_attn_b_log_gamma"].rearrange("(p o) -> p o", o=1))
                load(small[:, 3, 0:1], a["L0_attn_b_dt"].partition_broadcast(P))
                sp.wait_ge(setup_step, 1)
                for g in range(G):
                    rows = slice(HR * g, HR * g + DH)
                    load(wo_ret[rows, :, :],
                         a["L0_attn_a_wo"].rearrange("(t g d) n -> g d t n", g=G, d=DH)[g])
                    load(gn_w[rows, :], a["L0_attn_a_gn_w"][g])
                    load(gn_b[rows, :], a["L0_attn_a_gn_b"][g])
                sp.wait_ge(loaded, 16 * len(loads))

            n_loads = len(loads)

            @block.vector
            def _(dve):
                done = [0]

                def link(ins):
                    done[0] += 1
                    ins.then_inc(setup_step, 1)
                    dve.wait_ge(setup_step, done[0])

                dve.memset(gn_w[:], 0.0)
                dve.memset(gn_b[:], 0.0)
                link(dve.memset(wo_ret[:], 0.0))
                dve.memset(val[:], 0.0)
                dve.memset(Km[:].bitcast(F32), 0.0)
                link(dve.memset(neg_max[:].bitcast(F32), 0.0))
                link(dve.memset(val_heads[:, :, :, DEN:DEN + 1], 1.0))
                dve.wait_ge(loaded, 16 * n_loads)
                dve.tensor_copy(ident_r[:], ident[:])
                dve.tensor_copy(spread[:].rearrange("p a t n -> p (a t n)"),
                                hid[:, 0, :, :].rearrange("p c t -> p (c t)"))
                w1_f = probs[:, :, :, :].rearrange("p a g t -> p (a g) t")[:, 0:NE, :]
                link(dve.tensor_copy(w1_hi[:], w1_f))
                link(dve.tensor_tensor(w1_lo[:], w1_f, w1_hi[:].bitcast(F32), ALU.subtract))
                dve.tensor_scalar(nb_sgate[:], small[:, 0, 0:1], -1.0, None, ALU.mult)
                link(dve.tensor_scalar(small[:, 4, 0:1], small[:, 3, 0:1], -1.0, None, ALU.mult))
                link(dve.tensor_tensor(small[:, 4, 0:1], small[:, 4, 0:1], small[:, 3, 0:1], ALU.max))
                ang, turns, red = h[:, 0].rearrange("p t c -> p (t c)"), aT[:], tT
                link(dve.tensor_scalar(ang, ang, small[:, 1, 0:1], small[:, 4, 0:1], ALU.mult, ALU.mult))
                link(dve.tensor_scalar(turns, ang, 1.0 / (2 * np.pi), None, ALU.mult))
                link(dve.tensor_scalar(turns, turns, ROUND, None, ALU.add))
                link(dve.tensor_scalar(turns, turns, -ROUND, None, ALU.add))
                link(dve.scalar_tensor_tensor(red, turns, -TWO_PI_HI, ang, ALU.mult, ALU.add))
                link(dve.scalar_tensor_tensor(red, turns, -TWO_PI_LO, red, ALU.mult, ALU.add))
                link(dve.tensor_scalar(red, red, 3.1415925, -3.1415925, ALU.min, ALU.max))
                dve.wait_ge(setup_act, 3)
                link(dve.tensor_tensor(cos_t[:], cos_t[:], cos_t[:], ALU.mult))
                link(dve.tensor_scalar(cos_t[:], cos_t[:], -2.0, 1.0, ALU.mult, ALU.add))
                y, e, f = small[:, 6, 0:1], small[:, 6, 1:2], small[:, 6, 2:3]
                link(dve.tensor_tensor(y, small[:, 5, 0:1], small[:, 4, 0:1], ALU.mult))
                link(dve.tensor_scalar(y, y, 100.0, -1.0 / 256, ALU.min, ALU.mult))
                link(dve.memset(e, 1.0))
                for k in range(9, 1, -1):
                    link(dve.tensor_tensor(e, e, y, ALU.mult))
                    link(dve.tensor_scalar(e, e, 1.0 / k, 1.0, ALU.mult, ALU.add))
                link(dve.tensor_tensor(e, e, y, ALU.mult))
                for _ in range(8):
                    link(dve.tensor_scalar(f, e, 2.0, None, ALU.add))
                    link(dve.tensor_tensor(e, e, f, ALU.mult))
                link(dve.memset(rate[:], 1.0))
                link(dve.tensor_scalar(rate[:], rate[:], e, None, ALU.add))

            @block.scalar
            def _(act):
                act.wait_ge(loaded, 16 * n_loads)
                act.activation(small[:, 5, 0:1], small[:, 2, 0:1], ACT.Exp).then_inc(setup_act, 1)
                act.wait_ge(setup_step, 14)
                act.activation(sin_t[:], tT, ACT.Sin).then_inc(setup_act, 1)
                act.activation(cos_t[:], tT, ACT.Sin, scale=0.5).then_inc(setup_act, 1)

        FRONT_OF_RET = (0, 2)
        FRONT_OF_ATT = (1, 3, 4, 5)

        def keys_before(m):
            return sum(NG if k in FRONT_OF_RET else 1 for k in range(m))

        def keys_shared(m, t):
            return m in FRONT_OF_RET or t == 0

        def spread_bank(m, t, side):
            return ((X_BANK, 2), (0, 1))[t % 2 if m in FRONT_OF_RET else 0][side]

        def max_bank(i):
            return bank[MAX_BANKS[i % 2 if i < G * TT else (i - G * TT) % 3]]

        CELLS = {"ret": 7 + NH + 5, "att": 4 + G + 1 + NG * TT + 3, "scan": 9, "moe": 6 + 3 * (NE - 1) + 2}
        WINDOWS = ((("ret", 0), ("att", 0)), (("ret", 1), ("att", 1)),
                   (("scan", 0), ("att", 2)), (("scan", 1), ("att", 3)))

        def moe_of(window, first):
            if first and window == 0:
                return None
            return window - int(first), (1, 0, 1, 0)[window], (1, 0, 0, 1)[window]

        RET_BESIDE = [1, 0, 1, 1, 1, 1, 1] + [1, 1, 0, 1, 0, 1, 1, 0, 1, 0, 1, 1, 0, 1, 0, 0] + [1, 1, 1, 3, 0]
        SCAN_BESIDE = [1, 0, 2, 1, 2, 3, 2, 1, 3]
        ATT_BESIDE = {"ret": [3, 1, 1, 0, 1, 1, 1], "scan": [3, 2, 2, 2, 2, 1, 1, 1]}

        def beside(window):
            other = WINDOWS[window][0][0]
            counts = (RET_BESIDE if other == "ret" else SCAN_BESIDE) + ATT_BESIDE[other]
            cells = CELLS[other] + CELLS["att"]
            assert sum(counts) == CELLS["moe"]
            return counts + [0] * (cells - len(counts))

        def interleave(lane1, lane2, window, first):
            for count in beside(window):
                next(lane1)
                if moe_of(window, first):
                    for _ in range(count):
                        next(lane2)

        def both_lanes(stage, moe, first):
            for window in range(len(WINDOWS)):
                lane1 = (cell for kind, n in WINDOWS[window] for cell in stage(kind, n))
                m = moe_of(window, first)
                interleave(lane1, moe(*m) if m else iter(()), window, first)

        def newton_rsqrt(dve, link, v, tmp1, y):
            link(dve.tensor_scalar(y.bitcast(I32), v.bitcast(I32), 1, None, ALU.logical_shift_right))
            link(dve.tensor_scalar(y.bitcast(I32), y.bitcast(I32), -1.0, RSQRT_MAGIC, ALU.mult, ALU.add))
            for _ in range(3):
                link(dve.tensor_tensor(tmp1, y, y, ALU.mult))
                link(dve.scalar_tensor_tensor(tmp1, tmp1, 0.5, v, ALU.mult, ALU.mult))
                link(dve.scalar_tensor_tensor(y, tmp1, -1.5, y, ALU.add, ALU.mult))

        def layer_norm(dve, link, dst, src, st, means, tiny, dst2=None):
            for t in range(TT):
                last = dve.bn_stats(st[:, t, :], src[:, t, :])
            link(last)
            for t in range(TT):
                last = dve.bn_aggr(means[:, t, :], st[:, t, :])
            link(last)
            n = 2 * TT if dst2 is not None else TT
            v, tmp1, y = tiny[:, 0, 0:n], tiny[:, 1, 0:n], tiny[:, 2, 0:n]
            last = dve.tensor_scalar(v[:, 0:TT], means[:, 0:TT, 1], EPS, None, ALU.add)
            if dst2 is not None:
                last = dve.tensor_scalar(v[:, TT:n], means[:, 0:TT, 1], 1.0 + EPS, EPS * EPS, ALU.mult, ALU.add)
            link(last)
            newton_rsqrt(dve, link, v, tmp1, y)
            results = []
            for k, to in ((1, dst2), (0, dst)) if dst2 is not None else ((0, dst),):
                for t in range(TT):
                    last = dve.tensor_scalar(to[:, t, :], src[:, t, :], means[:, t, 0:1],
                                             y[:, TT * k + t:TT * k + t + 1], ALU.subtract, ALU.mult)
                results.append(last)
            return results if dst2 is not None else last

        def tensor_program(pe, first, only_moe=None):
            def transposes(dst, src):
                for t in range(TT):
                    last = pe.transpose(dst[:, t * P:(t + 1) * P], src[:, t, :], ident[:])
                return last

            def heads_kept(m, n_groups):
                pe.wait_ge(q_kept.sem, q_kept.at(m, n_groups))
                pe.wait_ge(k_kept.sem, k_kept.at(m, n_groups))
                pe.wait_ge(k_kept_v.sem, keys_before(m) + (n_groups if m in FRONT_OF_RET else 1))

            def spread_heads(m, t):
                behind = t - (2 if m in FRONT_OF_RET else 1)
                if behind >= 0:
                    heads_kept(m, behind + 1)
                for side in range(2):
                    dst = bank[spread_bank(m, t, side)]
                    pe.matmul(dst[:], spread[:, 2 * side, t, :], qk_hi[:, side, :], start=True, stop=False)
                    pe.matmul(dst[:], spread[:, 2 * side + 1, t, :], qk_lo[:, side, :],
                              start=False, stop=True).then_inc(spread_ready.sem, 1)

            def front(m, w):
                yield
                pe.wait_ge(normed.sem, normed.at(m, 1))
                transposes(bank[0], z_next if m in FRONT_OF_RET else zn).then_inc(normT.sem, 1)
                yield
                pe.wait_ge(aT_ready.sem, aT_ready.at(m, 1))
                if m == FRONT_OF_RET[1]:
                    pe.wait_ge(a_h.sem, a_h.at(0, 1))
                for i in range(2):
                    pe.matmul(bank[1 + i][:], w[:, i, :], aT[:], start=True, stop=True).then_inc(qkv_ready.sem, 1)
                for t in range(TT):
                    last = pe.matmul(bank[3][:, t * P:(t + 1) * P], aT[:, t * P:(t + 1) * P],
                                     w[:, 2, :], start=True, stop=True)
                last.then_inc(qkv_ready.sem, 1)
                yield
                pe.wait_ge(q_split.sem, q_split.at(m, 1))
                pe.wait_ge(k_split.sem, k_split.at(m, 1))
                spread_heads(m, 0)
                yield

            def values(kt, head):
                at = (kt * NH + head) * (DH + 1)
                return val[:, at:at + HR]

            def retention(n):
                m = FRONT_OF_RET[n]
                yield from front(m, w_ret)
                for t in range(1, NG):
                    spread_heads(m, t)
                    yield
                pe.wait_ge(v_ready.sem, v_ready.at(m, 1))
                heads_kept(m, NG)

                def scores_bank(u):
                    back = u - R_BANKS
                    if back >= 0:
                        if back % 3 == 0:
                            pe.wait_ge(r_diag.sem, r_diag.at(n, back // 3 + 1))
                        else:
                            pe.wait_ge(r_rest.sem, r_rest.at(n, 2 * (back // 3) + back % 3))
                    return bank[u % R_BANKS]

                def head_scores(head):
                    def product(dst, kt, queries):
                        return pe.matmul(dst, Km[:, head, P * kt:P * (kt + 1)], Qs[:, head // G, queries],
                                         start=True, stop=True)

                    dst = scores_bank(3 * head)
                    for kt in range(TT):
                        last = product(dst[:, P * kt:P * (kt + 1)], kt, slice(P * kt, P * (kt + 1)))
                    last.then_inc(r_scores.sem, 1)
                    dst = scores_bank(3 * head + 1)
                    product(dst[:, 0:T - P], 0, slice(P, T)).then_inc(r_scores.sem, 1)
                    dst = scores_bank(3 * head + 2)
                    product(dst[:, 0:2 * P], 1, slice(2 * P, T))
                    product(dst[:, 2 * P:3 * P], 2, slice(3 * P, T)).then_inc(r_scores.sem, 1)

                def sum_values(t, kt):
                    if kt == 0:
                        pe.wait_ge(r_diag.sem, r_diag.at(n, G * (t + 1)))
                        pe.wait_ge(r_rest.sem, r_rest.at(n, 2 * G * (t + 1)))
                        if t:
                            pe.wait_ge(r_kept.sem, r_kept.at(n, t))
                    for g in range(G):
                        last = pe.matmul(bank[X_BANK][HR * g:HR * (g + 1), P * kt:P * (kt + 1)],
                                         values(kt, G * t + g), probs[:, t % 2, g, P * kt:P * (kt + 1)],
                                         start=(kt == 0), stop=(kt in (0, TT - 1)), tile_position=(0, HR * g))
                    if kt == TT - 1:
                        last.then_inc(r_summed.sem, 1)
                        return
                    behind = (0, T - P, T + P)[kt]
                    for g in range(G):
                        pe.matmul(bank[X_BANK][HR * g:HR * (g + 1), P * (kt + 1):T], values(kt, G * t + g),
                                  r_behind[:, t % 2, g, behind:behind + T - P * (kt + 1)],
                                  start=(kt == 0), stop=False, tile_position=(0, HR * g))

                for head in range(NH):
                    head_scores(head)
                    if head >= G:
                        sum_values(head // G - 1, head % G)
                    yield
                for kt in range(TT):
                    sum_values(NG - 1, kt)
                yield
                pe.wait_ge(gn_local.sem, gn_local.at(n, 1))
                pe.matmul(bank[0][:, 0:2 * NG], average[:], mv[:, 0:NG, :].rearrange("p t s -> p (t s)"),
                          start=True, stop=True).then_inc(gn_mean.sem, 1)
                yield
                pe.wait_ge(gn_local.sem, gn_local.at(n, 2))
                pe.matmul(bank[1][:, 0:NG], average[:], gn[:, 2, :], start=True, stop=True).then_inc(gn_mean.sem, 1)
                yield
                yield
                pe.wait_ge(gn_done.sem, gn_done.at(n, NG))
                for tt in range(TT):
                    for t in range(NG):
                        last = pe.matmul(bank[2][:, P * tt:P * (tt + 1)], head_out[:, t, P * tt:P * (tt + 1)],
                                         wo_ret[:, t, :], start=(t == 0), stop=(t == NG - 1))
                last.then_inc(r_out.sem, 1)
                yield

            def attention(n):
                m = FRONT_OF_ATT[n]
                yield from front(m, w_qkv)

                def scores_for_max(head, qt):
                    i = head * TT + qt
                    if 2 <= i < G * TT + 2:
                        pe.wait_ge(a_max.sem, a_max.at(n, i - 1))
                    elif i > G * TT + 2:
                        pe.wait_ge(a_max.sem, a_max.at(n, i - 2))
                    pe.matmul(max_bank(i)[:], Qs[:, head // G, P * qt:P * (qt + 1)],
                              Km[:, head, :], start=True, stop=True).then_inc(a_scores.sem, 1)

                def queries_with_max(t):
                    pe.wait_ge(a_max.sem, a_max.at(n, TT * G * (t + 1)))
                    if t:
                        pe.wait_ge(a_qm_kept.sem, a_qm_kept.at(n, t))
                    if t >= 2:
                        pe.wait_ge(a_ctx.sem, a_ctx.at(n, t - 1))
                    pe.matmul(bank[QM_BANK][:], spread[:, 0, t, :], qk_hi[:, 0, :], start=True, stop=False)
                    pe.matmul(bank[QM_BANK][:], spread[:, 1, t, :], qk_lo[:, 0, :], start=False, stop=False)
                    for qt in range(TT):
                        last = pe.matmul(bank[QM_BANK][:, P * qt:P * (qt + 1)], neg_max[:, t % 2, qt, :],
                                         ident_r[:], start=False, stop=(qt == TT - 1))
                    last.then_inc(a_qm.sem, 1)

                def turn_out(t):
                    pe.wait_ge(a_kept.sem, a_kept.at(n, t + 1))
                    if t:
                        pe.wait_ge(a_ctx.sem, a_ctx.at(n, t))
                    for qt in range(TT):
                        last = pe.transpose(bank[TURN_BANK][:, P * qt:P * (qt + 1)],
                                            head_out[:, t, P * qt:P * (qt + 1)], ident[:])
                    last.then_inc(a_outT.sem, 1)

                def sum_values(step):
                    t, kt = step // TT, step % TT
                    pe.wait_ge(a_exp.sem, a_exp.at(n, G * (step + 1)))
                    if kt == 0 and t:
                        pe.wait_ge(a_kept.sem, a_kept.at(n, t))
                    for g in range(G):
                        last = pe.matmul(bank[X_BANK][HR * g:HR * (g + 1), :], values(kt, G * t + g),
                                         probs[:, step % 2, g, :], start=(kt == 0), stop=(kt == TT - 1),
                                         tile_position=(0, HR * g))
                    last.then_inc(a_pv.sem, 1)

                for head in range(G):
                    if head + 1 < NG:
                        spread_heads(m, head + 1)
                    if head == 0:
                        heads_kept(m, 1)
                    for qt in range(TT):
                        scores_for_max(head, qt)
                    yield
                pe.wait_ge(v_ready.sem, v_ready.at(m, 1))
                heads_kept(m, NG)
                if moe_of(n, first):
                    pe.wait_ge(m_acc.sem, m_acc.at(moe_of(n, first)[0], NE + 1))
                for qt in range(TT):
                    scores_for_max(G, qt)
                    if qt == 1:
                        queries_with_max(0)
                yield
                for step in range(NG * TT):
                    t, kt = step // TT, step % TT
                    if kt == 0:
                        pe.wait_ge(a_qm_kept.sem, a_qm_kept.at(n, t + 1))
                    for g in range(G):
                        i = step * G + g
                        if i >= len(S_BANKS):
                            pe.wait_ge(a_exp.sem, a_exp.at(n, i + 1 - len(S_BANKS)))
                        pe.matmul(bank[S_BANKS[i % 3]][:], Km[:, G * t + g, P * kt:P * (kt + 1)],
                                  Qs[:, t, :], start=True, stop=True).then_inc(a_scoresT.sem, 1)
                        if step + LEAD < NH:
                            scores_for_max(step + LEAD, g)
                        if g == 1 and step:
                            sum_values(step - 1)
                        if g == 1 and kt == TT - 1 and t + 1 < NG:
                            queries_with_max(t + 1)
                    if kt == 1 and t:
                        turn_out(t - 1)
                    yield
                sum_values(NG * TT - 1)
                turn_out(NG - 1)
                yield
                pe.wait_ge(a_ctx.sem, a_ctx.at(n, NG))
                transposes(bank[0], ctxt).then_inc(a_ctxT.sem, 1)
                yield
                pe.wait_ge(a_ctxT_kept.sem, a_ctxT_kept.at(n, 1))
                for tt in range(TT):
                    last = pe.matmul(bank[1][:, P * tt:P * (tt + 1)], ctxT[:, P * tt:P * (tt + 1)],
                                     w_o[:], start=True, stop=True)
                last.then_inc(a_proj.sem, 1)
                yield

            def scan(n):
                yield
                pe.wait_ge(s_normed.sem, s_normed.at(n, 1))
                transposes(bank[0], z_next).then_inc(s_normT.sem, 1)
                yield
                pe.wait_ge(s_aT.sem, s_aT.at(n, 1))
                pe.wait_ge(a_h.sem, a_h.at(1 + n, 1))
                pe.matmul(bank[3][:], w_sgate[:], aT[:], start=True, stop=True).then_inc(s_proj.sem, 1)
                for i in range(2):
                    pe.matmul(bank[1 + i][:], w_psi[:, P * i:P * (i + 1)], aT[:],
                              start=True, stop=True).then_inc(s_proj.sem, 1)
                yield
                pe.wait_ge(s_u.sem, s_u.at(n, 2))
                for tt in range(TT):
                    last = pe.matmul(bank[1 + tt // 2][:, 2 * P * (tt % 2):2 * P * (tt % 2 + 1)],
                                     aT[:, P * tt:P * (tt + 1)], w_phi[:], start=True, stop=True)
                last.then_inc(s_phi.sem, 1)
                yield
                yield
                yield
                for i in range(2):
                    pe.wait_ge(s_h.sem, s_h.at(n, i + 1))
                    for tt in range(TT):
                        last = pe.transpose(bank[3 + i][:, P * tt:P * (tt + 1)],
                                            U[i][:, P * tt:P * (tt + 1)], ident[:])
                    last.then_inc(s_hT.sem, 1)
                yield
                yield
                yield

            def experts_stage(r, s, layer):
                def hidden(e):
                    for c in range(HC):
                        i = e * HC + c
                        if i >= 2:
                            pe.wait_ge(m_gelu.sem, m_gelu.at(r, i - 1))
                        cols = slice(P * c, P * (c + 1))
                        dst = bank[H_BANK + i % 2]
                        pe.matmul(dst[:], w1_hi[:, e, cols], t_hi[:], start=True, stop=False)
                        pe.matmul(dst[:], w1_hi[:, e, cols], t_lo[:], start=False, stop=False)
                        pe.matmul(dst[:], w1_lo[:, e, cols], t_hi[:], start=False,
                                  stop=True).then_inc(m_hid.sem, 1)

                yield
                pe.wait_ge(m_normed.sem, m_normed.at(r, 1))
                transposes(bank[O_BANK], tn).then_inc(m_normT.sem, 1)
                yield
                pe.wait_ge(m_tT.sem, m_tT.at(r, 1))
                for tt in range(TT):
                    last = pe.matmul(bank[O_BANK][:, NE * tt:NE * (tt + 1)], tT[:, P * tt:P * (tt + 1)],
                                     w_gate[:], start=True, stop=True)
                last.then_inc(m_logits.sem, 1)
                yield
                pe.wait_ge(m_split.sem, m_split.at(r, 1))
                hidden(0)
                yield
                pe.wait_ge(m_we.sem, m_we.at(r, 1))
                for tt in range(TT):
                    last = pe.transpose(bank[O_BANK][0:NE, P * tt:P * (tt + 1)], we[:, tt, :], ident[:])
                last.then_inc(m_weT.sem, 1)
                yield
                pe.wait_ge(m_weT_kept.sem, m_weT_kept.at(r, 1))
                for tt in range(TT):
                    last = pe.matmul(bank[O_BANK][:, P * tt:P * (tt + 1)], weT[:, P * tt:P * (tt + 1)],
                                     b2[:], start=True, stop=True)
                last.then_inc(m_bias.sem, 1)
                yield

                def output(e, half):
                    if half == 0:
                        pe.wait_ge(m_gelu.sem, m_gelu.at(r, HC * (e + 1)))
                        pe.wait_ge(m_acc.sem, m_acc.at(r, e + 1))
                    for tt in range(TT // 2 * half, TT // 2 * (half + 1)):
                        for c in range(HC):
                            last = pe.matmul(bank[O_BANK][:, P * tt:P * (tt + 1)],
                                             hid[:, e % 2, c, P * tt:P * (tt + 1)],
                                             w2[:, e * HC + c, :], start=(c == 0), stop=(c == HC - 1))
                    if half == 1:
                        last.then_inc(m_out.sem, 1)

                for e in range(1, NE):
                    hidden(e)
                    yield
                    for half in range(2):
                        output(e - 1, half)
                        yield
                for half in range(2):
                    output(NE - 1, half)
                    yield

            if only_moe:
                for _ in experts_stage(*only_moe):
                    pass
            else:
                both_lanes(lambda kind, n: {"ret": retention, "att": attention, "scan": scan}[kind](n),
                           experts_stage, first)

        def scalar_program(act, first, only_moe=None):
            def keep_heads(m, t):
                act.wait_ge(spread_ready.sem, spread_ready.at(m, 2 * t + 1))
                act.copy(Qs[:, t, :], bank[spread_bank(m, t, 0)][:]).then_inc(q_kept.sem, 1)
                act.wait_ge(spread_ready.sem, spread_ready.at(m, 2 * t + 2))
                for g in range(0, G // 2 if keys_shared(m, t) else G):
                    rows = slice(HR * g, HR * (g + 1))
                    last = act.activation(Km[rows, G * t + g, :], bank[spread_bank(m, t, 1)][rows, :],
                                          ACT.Identity, bias=ones_row[rows, :])
                last.then_inc(k_kept.sem, 1)

            def front(m, n):
                yield
                act.wait_ge(normT.sem, normT.at(m, 1))
                if m in FRONT_OF_RET:
                    act.copy(aT[:], bank[0][:]).then_inc(aT_ready.sem, 1)
                else:
                    act.activation(aT[:], bank[0][:], ACT.Identity,
                                   bias=ln_wb[:, 1:2], scale=ln_wb[:, 0:1]).then_inc(aT_ready.sem, 1)
                yield
                if m not in FRONT_OF_RET:
                    for i in range(2):
                        act.wait_ge(qkv_ready.sem, qkv_ready.at(m, i + 1))
                        act.activation(qk_f[:, i, :], bank[1 + i][:], ACT.Identity,
                                       bias=b_qk[:, i:i + 1]).then_inc(qk_biased.sem, 1)
                yield
                keep_heads(m, 0)
                yield

            def retention(n):
                m = FRONT_OF_RET[n]
                yield from front(m, n)
                for t in range(1, NG):
                    keep_heads(m, t)
                    yield

                def keep(t):
                    act.wait_ge(r_summed.sem, r_summed.at(n, t + 1))
                    act.copy(head_out[:, t, :], bank[X_BANK][:]).then_inc(r_kept.sem, 1)

                for head in range(NH):
                    t, g = head // G, head % G
                    if g == 0 and t >= 2:
                        keep(t - 2)
                    for j in range(2):
                        u = 3 * head + 1 + j
                        act.wait_ge(r_scores.sem, r_scores.at(n, u + 1))
                        act.copy(r_behind[:, t % 2, g, (T - P) * j:(T - P) * (j + 1)],
                                 bank[u % R_BANKS][:, 0:T - P]).then_inc(r_rest.sem, 1)
                    yield
                keep(NG - 2)
                keep(NG - 1)
                yield
                yield
                yield
                yield
                yield

            def attention(n):
                m = FRONT_OF_ATT[n]
                yield from front(m, n)

                def keep_queries(t):
                    act.wait_ge(a_qm.sem, a_qm.at(n, t + 1))
                    act.copy(Qs[:, t, :], bank[QM_BANK][:]).then_inc(a_qm_kept.sem, 1)

                def keep_sums(t):
                    act.wait_ge(a_pv.sem, a_pv.at(n, TT * (t + 1)))
                    act.copy(head_out[:, t, :], bank[X_BANK][:]).then_inc(a_kept.sem, 1)

                for t in range(G):
                    if t + 1 < NG:
                        keep_heads(m, t + 1)
                    yield
                keep_queries(0)
                yield
                for step in range(NG * TT):
                    t, kt = step // TT, step % TT
                    for g in range(G):
                        i = step * G + g
                        act.wait_ge(a_scoresT.sem, a_scoresT.at(n, i + 1))
                        if g == 0 and step >= 2:
                            act.wait_ge(a_pv.sem, a_pv.at(n, step - 1))
                        act.activation(probs[:, step % 2, g, :], bank[S_BANKS[i % 3]][:],
                                       ACT.Exp, scale=SCALE).then_inc(a_exp.sem, 1)
                        if g == 1 and kt == TT - 1 and t + 1 < NG:
                            keep_queries(t + 1)
                    if kt == 0 and t:
                        keep_sums(t - 1)
                    yield
                keep_sums(NG - 1)
                yield
                act.wait_ge(a_ctxT.sem, a_ctxT.at(n, 1))
                act.copy(ctxT[:], bank[0][:]).then_inc(a_ctxT_kept.sem, 1)
                yield
                yield

            def scan(n):
                yield
                act.wait_ge(s_normT.sem, s_normT.at(n, 1))
                act.copy(aT[:], bank[0][:]).then_inc(s_aT.sem, 1)
                yield
                act.wait_ge(s_proj.sem, s_proj.at(n, 1))
                act.activation(sig, bank[3][:], ACT.Exp, bias=nb_sgate[:], scale=-1.0).then_inc(s_gexp.sem, 1)
                yield
                for _ in range(6):
                    yield

            def experts_stage(r, s, layer):
                yield
                act.wait_ge(m_normT.sem, m_normT.at(r, 1))
                act.activation(tT, bank[O_BANK][:], ACT.Identity,
                               bias=ln_wb[:, 3:4], scale=ln_wb[:, 2:3]).then_inc(m_tT.sem, 1)
                yield
                yield
                act.wait_ge(m_gap.sem, m_gap.at(r, 1))
                act.activation(gw[:, 1, :], gw[:, 0, :], ACT.Exp).then_inc(m_gap_exp.sem, 1)
                for e in range(NE):
                    for c in range(HC):
                        i = e * HC + c
                        act.wait_ge(m_hid.sem, m_hid.at(r, i + 1))
                        if c == 0 and e >= 2:
                            act.wait_ge(m_out.sem, m_out.at(r, e - 1))
                        act.activation(hid[:, e % 2, c, :], bank[H_BANK + i % 2][:],
                                       ACT.Gelu_apprx_tanh, bias=b1[:, i:i + 1]).then_inc(m_gelu.sem, 1)
                    yield
                    yield
                    yield
                yield
                yield

            if only_moe:
                for _ in experts_stage(*only_moe):
                    pass
            else:
                both_lanes(lambda kind, n: {"ret": retention, "att": attention, "scan": scan}[kind](n),
                           experts_stage, first)

        def vector_program(dve, first, only_moe=None):
            steps = [0]

            def link(ins):
                steps[0] += 1
                ins.then_inc(vec_step, 1)
                dve.wait_ge(vec_step, steps[0])

            def keep_keys(m, t):
                dve.wait_ge(spread_ready.sem, spread_ready.at(m, 2 * t + 2))
                for g in range(G // 2, G):
                    rows = slice(HR * g, HR * (g + 1))
                    last = dve.tensor_scalar(Km[rows, G * t + g, :], bank[spread_bank(m, t, 1)][rows, :],
                                             ones_row[rows, :], None, ALU.add)
                last.then_inc(k_kept_v.sem, 1)

            def norm_ahead(window):
                kind, s = WINDOWS[window][0]
                if kind == "ret":
                    dve.wait_ge(x_in[s], 16)
                else:
                    dve.wait_ge(m_acc.sem, m_acc.at(moe_of(1 + s, first)[0], NE + 1))
                done = normed if kind == "ret" else s_normed
                layer_norm(dve, link, z_next, x[:, s], stat, mv, small).then_inc(done.sem, 1)

            def front(m, s):
                if m not in FRONT_OF_RET:
                    twice, once = layer_norm(dve, link, z, x[:, s], stat, mv, small, zn)
                    twice.then_inc(normed.sem, 1)
                    once.then_inc(a_z.sem, 1)
                elif s == 0:
                    norm_ahead(0)
                yield
                yield
                for i in range(2):
                    if m in FRONT_OF_RET:
                        dve.wait_ge(qkv_ready.sem, qkv_ready.at(m, i + 1))
                        link(dve.tensor_tensor(qk_f[:, i, :], bank[1 + i][:], qk_decay[:, i, :], ALU.mult))
                    else:
                        dve.wait_ge(qk_biased.sem, qk_biased.at(FRONT_OF_ATT.index(m), i + 1))
                    high = dve.tensor_copy(qk_hi[:, i, :], qk_f[:, i, :])
                    if i == 0:
                        high.then_inc(q_hi.sem, 1)
                    else:
                        link(high)
                        dve.tensor_tensor(qk_lo[:, 1, :], qk_f[:, 1, :], qk_hi[:, 1, :].bitcast(F32),
                                          ALU.subtract).then_inc(k_split.sem, 1)
                dve.wait_ge(qkv_ready.sem, qkv_ready.at(m, 3))
                src = bank[3][:].rearrange("p (t h d) -> p t h d", t=TT, h=NH)
                if m in FRONT_OF_RET:
                    dve.tensor_copy(val_heads[:, :, :, 0:DH], src).then_inc(v_ready.sem, 1)
                else:
                    for t in range(TT):
                        last = dve.tensor_tensor(val_heads[:, t, :, 0:DH], src[:, t],
                                                 b_v[:].rearrange("p (h d) -> p h d", h=NH), ALU.add)
                    last.then_inc(v_ready.sem, 1)
                yield
                keep_keys(m, 0)
                yield

            def retention(n):
                m = FRONT_OF_RET[n]
                yield from front(m, n)
                for t in range(1, NG):
                    keep_keys(m, t)
                    yield
                for head in range(NH):
                    t, g = head // G, head % G
                    if g == 0 and t >= 2:
                        dve.wait_ge(r_kept.sem, r_kept.at(n, t - 1))
                        dve.bn_stats(stat[:, t - 2, :], head_out[:, t - 2, :])
                    dve.wait_ge(r_scores.sem, r_scores.at(n, 3 * head + 1))
                    dve.tensor_tensor(probs[:, t % 2, g, :].rearrange("p (k q) -> p k q", k=TT),
                                      bank[3 * head % R_BANKS][:].rearrange("p (k q) -> p k q", k=TT),
                                      causal[:].unsqueeze(1).broadcast_to([P, TT, P]),
                                      ALU.mult).then_inc(r_diag.sem, 1)
                    yield
                for t in (NG - 2, NG - 1):
                    dve.wait_ge(r_kept.sem, r_kept.at(n, t + 1))
                    last = dve.bn_stats(stat[:, t, :], head_out[:, t, :])
                link(last)
                yield
                for t in range(NG):
                    last = dve.bn_aggr(mv[:, t, :], stat[:, t, :])
                last.then_inc(gn_local.sem, 1)
                yield
                dve.wait_ge(gn_mean.sem, gn_mean.at(n, 1))
                link(dve.tensor_copy(gn[:, 0:2, :], bank[0][:, 0:2 * NG].rearrange("p (t s) -> p s t", s=2)))
                link(dve.tensor_tensor(gn[:, 2, :], mv[:, 0:NG, 0], gn[:, 0, :], ALU.subtract))
                dve.tensor_tensor(gn[:, 2, :], gn[:, 2, :], gn[:, 2, :], ALU.mult).then_inc(gn_local.sem, 1)
                yield
                dve.wait_ge(gn_mean.sem, gn_mean.at(n, 2))
                v = small[:, 0, 0:NG]
                link(dve.scalar_tensor_tensor(v, gn[:, 1, :], EPS, bank[1][:, 0:NG], ALU.add, ALU.add))
                newton_rsqrt(dve, link, v, small[:, 1, 0:NG], gn[:, 3, :])
                link(dve.tensor_tensor(gn[:, 4, :], gn[:, 3, :], gn_w[:], ALU.mult))
                link(dve.tensor_tensor(small[:, 0, 0:NG], gn[:, 0, :], gn[:, 4, :], ALU.mult))
                link(dve.tensor_tensor(gn[:, 5, :], gn_b[:], small[:, 0, 0:NG], ALU.subtract))
                for t in range(NG):
                    dve.tensor_scalar(head_out[:, t, :], head_out[:, t, :], gn[:, 4, t:t + 1],
                                      gn[:, 5, t:t + 1], ALU.mult, ALU.add).then_inc(gn_done.sem, 1)
                yield
                dve.wait_ge(r_out.sem, r_out.at(n, 1))
                xf = x[:, n].rearrange("p t c -> p (t c)")
                link(dve.tensor_tensor(xf, bank[2][:], xf, ALU.add))
                yield

            def attention(n):
                m, s = FRONT_OF_ATT[n], n % 2
                yield from front(m, s)

                def maxima(head):
                    t, g = head // G, head % G
                    if g == 0 and t >= 2:
                        dve.wait_ge(a_qm.sem, a_qm.at(n, t - 1))
                    for qt in range(TT):
                        i = head * TT + qt
                        dve.wait_ge(a_scores.sem, a_scores.at(n, i + 1))
                        col = HR * g + MAX_ROW
                        dve.tensor_reduce(neg_max[:, t % 2, qt, col:col + 1], max_bank(i)[:],
                                          AX_X, ALU.max, negate=True).then_inc(a_max.sem, 1)

                def normalise(t):
                    dve.wait_ge(a_outT.sem, a_outT.at(n, t + 1))
                    if t:
                        dve.wait_ge(a_ctx.sem, a_ctx.at(n, t))
                    else:
                        dve.wait_ge(a_zb.sem, a_zb.at(n, 1))
                    src = bank[TURN_BANK][:].rearrange("p (q g r) -> p q g r", q=TT, g=G)
                    link(dve.reciprocal(rden[:], src[:, :, :, DEN]))
                    dst = ctxt[:, :, C // NG * t:C // NG * (t + 1)].rearrange("p q (g d) -> p q g d", g=G)
                    dve.tensor_tensor(dst, src[:, :, :, 0:DH], rden[:].unsqueeze(3).broadcast_to([P, TT, G, DH]),
                                      ALU.mult).then_inc(a_ctx.sem, 1)

                for head in range(LEAD):
                    maxima(head)
                    yield
                for step in range(NG * TT):
                    t, kt = step // TT, step % TT
                    if step + LEAD < NH:
                        maxima(step + LEAD)
                    if kt == 1 and t:
                        normalise(t - 1)
                    if step + LEAD == NH and n + 1 < len(WINDOWS):
                        norm_ahead(n + 1)
                    yield
                normalise(NG - 1)
                yield
                yield
                dve.wait_ge(a_proj.sem, a_proj.at(n, 1))
                hf = h[:, s].rearrange("p t c -> p (t c)")
                dve.tensor_tensor(hf, bank[1][:], hf, ALU.add).then_inc(a_h.sem, 1)
                yield

            def scan(n):
                xs = x[:, n]
                yield
                yield
                dve.wait_ge(s_gexp.sem, s_gexp.at(n, 1))
                link(dve.tensor_scalar(sig, sig, 1.0, None, ALU.add))
                link(dve.reciprocal(sig, sig))
                for i in range(2):
                    dve.wait_ge(s_proj.sem, s_proj.at(n, 2 + i))
                    dve.scalar_tensor_tensor(U[i], bank[1 + i][:], b_psi[:, i:i + 1], sig,
                                             ALU.add, ALU.mult).then_inc(s_u.sem, 1)
                dve.wait_ge(s_u.sem, s_u.at(n, 2))
                yield
                dve.tensor_tensor(tmp[0], U[0], cos_t[:], ALU.mult)
                dve.tensor_tensor(tmp[1], U[1], sin_t[:], ALU.mult)
                dve.tensor_tensor(W[0], U[1], cos_t[:], ALU.mult)
                link(dve.tensor_tensor(W[1], U[0], sin_t[:], ALU.mult))
                dve.tensor_tensor(rot[0], tmp[0], tmp[1], ALU.add)
                link(dve.tensor_tensor(rot[1], W[0], W[1], ALU.subtract))
                yield
                dve.tensor_tensor_scan(W[0], rate[:].broadcast_to([P, T]), rot[0], 0.0, ALU.mult, ALU.add)
                link(dve.tensor_tensor_scan(W[1], rate[:].broadcast_to([P, T]), rot[1], 0.0, ALU.mult, ALU.add))
                yield
                dve.tensor_tensor(tmp[0], W[0], cos_t[:], ALU.mult)
                dve.tensor_tensor(tmp[1], W[1], sin_t[:], ALU.mult)
                dve.tensor_tensor(rot[0], W[0], sin_t[:], ALU.mult)
                link(dve.tensor_tensor(rot[1], W[1], cos_t[:], ALU.mult))
                dve.tensor_tensor(U[0], tmp[0], tmp[1], ALU.subtract).then_inc(s_h.sem, 1)
                dve.tensor_tensor(U[1], rot[0], rot[1], ALU.add).then_inc(s_h.sem, 1)
                yield
                dve.wait_ge(s_phi.sem, s_phi.at(n, 1))
                for i in range(2):
                    last = dve.tensor_tensor(phi[:, 2 * i:2 * i + 2, :],
                                             bank[1 + i][:].rearrange("p (t e) -> p t e", t=2),
                                             b_phi[:].unsqueeze(1).broadcast_to([P, 2, 2 * P]), ALU.add)
                yield
                dve.wait_ge(s_hT.sem, s_hT.at(n, 2))
                for i in range(2):
                    for t in range(TT):
                        last = dve.bn_stats(stat[:, TT * i + t, :], bank[3 + i][:, P * t:P * (t + 1)])
                link(last)
                for j in range(2 * TT):
                    last = dve.bn_aggr(mv[:, j, :], stat[:, j, :])
                link(last)
                v, t1, y = small[:, 0, :], small[:, 1, :], small[:, 2, :]
                link(dve.tensor_scalar(v, mv[:, :, 1], TINY, None, ALU.add))
                newton_rsqrt(dve, link, v, t1, y)
                link(dve.tensor_tensor(y, y, mv[:, :, 1], ALU.mult))
                link(dve.tensor_scalar(y, y, PROJ_EPS, None, ALU.add))
                link(dve.reciprocal(y, y))
                yield
                for i in range(2):
                    for t in range(TT):
                        j = TT * i + t
                        last = dve.tensor_scalar(Hn[:, i, t, :], bank[3 + i][:, P * t:P * (t + 1)],
                                                 mv[:, j, 0:1], y[:, j:j + 1], ALU.subtract, ALU.mult)
                link(last)
                for i in range(2):
                    last = dve.tensor_tensor(Hn[:, i], Hn[:, i], phi[:, :, P * i:P * (i + 1)], ALU.mult)
                link(last)
                link(dve.tensor_tensor(Hn[:, 0], Hn[:, 0], Hn[:, 1], ALU.add))
                link(dve.tensor_tensor(xs, xs, Hn[:, 0], ALU.add))
                yield

            def experts_stage(r, s, layer):
                if not (layer == 1 and s == 1):
                    dve.wait_ge(a_h.sem, a_h.at(s + 2 * layer, 1))
                layer_norm(dve, link, tn, h[:, s], m_stat, m_mv, m_small).then_inc(m_normed.sem, 1)
                yield
                yield
                dve.wait_ge(m_tT.sem, m_tT.at(r, 1))
                dve.tensor_copy(t_hi[:], tT).then_inc(m_hi.sem, 1)
                dve.wait_ge(m_logits.sem, m_logits.at(r, 1))
                link(dve.tensor_copy(logits[:].rearrange("p t e -> p (t e)"), bank[O_BANK][:, 0:TT * NE]))
                for t in range(TT):
                    last = dve.max(top[:, t, :], logits[:, t, :])
                link(last)
                for t in range(TT):
                    last = dve.max_index(top_i[:, t, :], top[:, t, :], logits[:, t, :])
                dve.tensor_tensor(gw[:, 0, :], top[:, :, 1], top[:, :, 0], ALU.subtract).then_inc(m_gap.sem, 1)
                yield
                dve.wait_ge(m_gap.sem, m_gap.at(r, 1))
                link(dve.tensor_copy(top_f[:], top_i[:]))
                for k in range(2):
                    last = dve.tensor_tensor(hot[:, k], experts[:],
                                             top_f[:, :, k:k + 1].broadcast_to([P, TT, NE]), ALU.is_equal)
                dve.wait_ge(m_gap_exp.sem, m_gap_exp.at(r, 1))
                link(last)
                link(dve.tensor_scalar(gw[:, 2, :], gw[:, 1, :], 1.0, None, ALU.add))
                link(dve.reciprocal(gw[:, 2, :], gw[:, 2, :]))
                link(dve.tensor_tensor(gw[:, 3, :], gw[:, 1, :], gw[:, 2, :], ALU.mult))
                for k in range(2):
                    last = dve.tensor_tensor(hot[:, k], hot[:, k],
                                             gw[:, 2 + k, :].unsqueeze(2).broadcast_to([P, TT, NE]), ALU.mult)
                link(last)
                dve.tensor_tensor(we[:], hot[:, 0], hot[:, 1], ALU.add).then_inc(m_we.sem, 1)
                yield
                dve.wait_ge(m_weT.sem, m_weT.at(r, 1))
                dve.tensor_copy(weT[:], bank[O_BANK][0:NE, :]).then_inc(m_weT_kept.sem, 1)
                yield
                dve.wait_ge(m_bias.sem, m_bias.at(r, 1))
                if not (layer == 1 and s == 1):
                    dve.wait_ge(a_xh.sem, a_xh.at(s + 2 * layer, 1))
                xf = x[:, s].rearrange("p t c -> p (t c)")
                dve.tensor_tensor(xf, bank[O_BANK][:], xf, ALU.add).then_inc(m_acc.sem, 1)
                yield

                def weigh(e):
                    dve.wait_ge(m_out.sem, m_out.at(r, e + 1))
                    dve.wait_ge(m_acc.sem, m_acc.at(r, e + 1))
                    for t in range(TT):
                        last = dve.scalar_tensor_tensor(x[:, s, t, :], bank[O_BANK][:, P * t:P * (t + 1)],
                                                        we[:, t, e:e + 1], x[:, s, t, :], ALU.mult, ALU.add)
                    last.then_inc(m_acc.sem, 1)

                for e in range(1, NE):
                    yield
                    yield
                    weigh(e - 1)
                    yield
                yield
                weigh(NE - 1)
                yield

            if only_moe:
                for _ in experts_stage(*only_moe):
                    pass
            else:
                both_lanes(lambda kind, n: {"ret": retention, "att": attention, "scan": scan}[kind](n),
                           experts_stage, first)

        def pool_program(pool, first, only_moe=None):
            def split_tokens(r):
                pool.wait_ge(m_hi.sem, m_hi.at(r, 1))
                pool.tensor_tensor(t_lo[:], tT, t_hi[:].bitcast(F32), ALU.subtract).then_inc(m_split.sem, 1)

            if only_moe:
                split_tokens(only_moe[0])
                return

            def split_queries(m):
                pool.wait_ge(q_hi.sem, q_hi.at(m, 1))
                pool.tensor_tensor(qk_lo[:, 0, :], qk_f[:, 0, :], qk_hi[:, 0, :].bitcast(F32),
                                   ALU.subtract).then_inc(q_split.sem, 1)

            for n in range(4):
                s = n % 2
                if WINDOWS[n][0][0] == "ret":
                    split_queries(FRONT_OF_RET[n])
                if moe_of(n, first):
                    split_tokens(moe_of(n, first)[0])
                pool.wait_ge(a_z.sem, a_z.at(n, 1))
                pool.tensor_tensor(h[:, s], z[:], b_o[:].unsqueeze(1).broadcast_to([P, TT, C]),
                                   ALU.add).then_inc(a_zb.sem, 1)
                split_queries(FRONT_OF_ATT[n])
                pool.wait_ge(a_h.sem, a_h.at(n, 1))
                pool.tensor_tensor(x[:, s], x[:, s], h[:, s], ALU.add).then_inc(a_xh.sem, 1)

        def sync_program(sp, pair, first):
            def tokens(dram, b):
                return dram[b].rearrange("(t p) c -> p t c", p=P)

            sp.dma_start(x[:, 0], tokens(a["x"], 2 * pair)).then_inc(x_in[0], 16)
            if not first:
                sp.wait_ge(m_acc.sem, m_acc.at(0, NE + 1))
                sp.dma_start(tokens(out, 2 * pair - 1), x[:, 1]).then_inc(stored_it, 16)
                sp.wait_ge(stored_it, 16)
            sp.dma_start(x[:, 1], tokens(a["x"], 2 * pair + 1)).then_inc(x_in[1], 16)
            sp.wait_ge(m_acc.sem, m_acc.at(3 - int(first), NE + 1))
            sp.dma_start(tokens(out, 2 * pair), x[:, 0]).then_inc(stored_it, 16)
            sp.wait_ge(stored_it, 16 if first else 32)

        def restart():
            nums = sorted(s.num for s in sems)
            assert nums == list(range(nums[0], nums[-1] + 1))
            nc.all_engine_barrier(sems_to_clear=range(nums[0], nums[-1] + 1))

        def one_pair(pair, first):
            with nc.Block() as block:
                @block.sync
                def _(sp):
                    sync_program(sp, pair, first)

                @block.gpsimd
                def _(pool):
                    pool_program(pool, first)

                @block.tensor
                def _(pe):
                    tensor_program(pe, first)

                @block.scalar
                def _(act):
                    scalar_program(act, first)

                @block.vector
                def _(dve):
                    vector_program(dve, first)
            restart()

        one_pair(0, True)
        with nc.Fori(1, B // 2) as pair:
            one_pair(pair, False)

        last_moe = (0, 1, 1)
        with nc.Block() as block:
            @block.gpsimd
            def _(pool):
                pool_program(pool, False, last_moe)

            @block.tensor
            def _(pe):
                tensor_program(pe, False, last_moe)

            @block.scalar
            def _(act):
                scalar_program(act, False, last_moe)

            @block.vector
            def _(dve):
                vector_program(dve, False, last_moe)

            @block.sync
            def _(sp):
                sp.wait_ge(m_acc.sem, m_acc.at(0, NE + 1))
                sp.dma_start(out[B - 1].rearrange("(t p) c -> p t c", p=P), x[:, 1]).then_inc(stored_it, 16)
                sp.wait_ge(stored_it, 16)


_TRANSPOSED = ("L0_attn_a_wq", "L0_attn_a_wk", "L0_attn_a_wv", "L0_attn_a_wo",
               "L0_attn_b_W_psi", "L0_attn_b_W_phi", "L0_attn_b_W_gate")


def kernel(**inputs):
    import concourse.bacc as _bacc
    from concourse.bass_utils import run_bass_kernel_spmd as _run

    nc = _bacc.Bacc("TRN2", target_bir_lowering=False, num_devices=1)
    arrays = {}
    for name, v in inputs.items():
        v = np.asarray(v)
        if name == "L0_attn_a_x":
            name = "x"
        if name in _TRANSPOSED:
            v = v.T
        if name in ("L0_ffn_b1", "L0_attn_b_b_psi"):
            v = v.reshape(-1, P).T
        if name in ("L0_attn_a_gn_w", "L0_attn_a_gn_b"):
            v = v.reshape(NG, G, DH).transpose(1, 2, 0)
        if v.ndim == 0:
            v = v.reshape(1)
        arrays[name] = np.ascontiguousarray(v)
    arrays.update(shape_constants())
    aps = {name: nc.dram_tensor("in_" + name, v.shape, F32, kind="ExternalInput").ap()
           for name, v in arrays.items()}
    out = nc.dram_tensor("out", (B, T, C), F32, kind="ExternalOutput").ap()
    build(nc, aps, out)
    r = _run(nc, [{"in_" + name: v for name, v in arrays.items()}], core_ids=[0])
    return r.results[0]["out"]
```
